# Optimizing a Trainium2 kernel written in Bass

```python
import numpy as np
import jax
import jax.numpy as jnp

def _softmax(x, axis=-1):
    return jax.nn.softmax(x, axis=axis)
def _gelu(x):
    return jax.nn.gelu(x, approximate=True)
def _silu(x):
    return jax.nn.silu(x)
def _sigmoid(x):
    return jax.nn.sigmoid(x)
def _layernorm(x, axis=-1, eps=1e-5):
    m = jnp.mean(x, axis=axis, keepdims=True)
    v = jnp.var(x, axis=axis, keepdims=True)
    return (x - m) / jnp.sqrt(v + eps)
def _scatter_add(tgt, idx, src, axis=0):
    return tgt.at[idx].add(src)
def _segment_sum(src, seg, n):
    return jax.ops.segment_sum(src, seg, n)

kernel_name = 'mk_adj_resnorm_d4_adj_512_766617'

def setup_inputs(seed: int = 0):
    np.random.seed(seed)
    _w = jnp.asarray
    def _rec_inputs():
        import jax
        import jax.numpy as jnp
        _gk = jax.random.key(seed)
        x = -0.0005207 + 1.001 * jax.random.normal(jax.random.fold_in(_gk, 1), (4096, 512), jnp.float32)
        _a = jax.random.bernoulli(jax.random.fold_in(_gk, 2), 0.0078125, (4096, 4096))
        _a = jnp.logical_or(_a, jnp.swapaxes(_a, -1, -2))
        _a = jnp.logical_or(_a, jnp.eye(4096, dtype=bool))
        adj = _a.astype(jnp.int32)
        return x, adj
    x, adj = _rec_inputs()
    def _L0_gnn_setup():
        import jax, jax.numpy as jnp
        import numpy as np
        N, IN, OUT, H = (4096, 512, 64, 8)
        ALPHA = 0.2
        NEG = -9000000000000000.0

        def glorot(key, shape):
            fan_in, fan_out = (shape[-2], shape[-1])
            limit = np.sqrt(6.0 / (fan_in + fan_out))
            return jax.random.uniform(key, shape, jnp.float32, -limit, limit)
        key = jax.random.key(seed)
        k1, k2, k3, k4, k5 = jax.random.split(key, 5)
        x = jax.random.normal(k1, (N, IN), jnp.float32)
        adj = jax.random.randint(k2, (N, N), 0, 2, jnp.int32)
        W = glorot(k3, (H, IN, OUT))
        a1 = glorot(k4, (H, OUT, 1))[..., 0]
        a2 = glorot(k5, (H, OUT, 1))[..., 0]
        return {'x': x, 'adj': adj, 'W': W, 'a1': a1, 'a2': a2}
    _L0_gnn_all = _L0_gnn_setup()
    _L0_gnn_in = {k: v for k, v in _L0_gnn_all.items() if k in ('W', 'a1', 'a2', )}
    del _L0_gnn_all

    def _L1_gnn_setup():
        import jax, jax.numpy as jnp
        import numpy as np
        N, IN, H, D = (4096, 512, 8, 64)
        ALPHA = 0.2
        NEG_BIG = -9000000000000000.0
        key = jax.random.key(seed)
        k1, k2, k3, k4 = jax.random.split(key, 4)
        h = jax.random.normal(k1, (N, IN), dtype=jnp.float32)
        adj = jax.random.randint(k2, (N, N), 0, 2, dtype=jnp.int32)
        W = jax.random.normal(k3, (IN, H * D), dtype=jnp.float32) * (1.0 / np.sqrt(IN))
        a = jax.random.normal(k4, (1, H, 2 * D), dtype=jnp.float32)
        return {'h': h, 'adj': adj, 'W': W, 'a': a}
    _L1_gnn_all = _L1_gnn_setup()
    _L1_gnn_in = {k: v for k, v in _L1_gnn_all.items() if k in ('W', 'a', )}
    del _L1_gnn_all

    def _L2_gnn_setup():
        import jax, jax.numpy as jnp
        import numpy as np
        NEG_SLOPE = 0.2
        N, IN_DIM, OUT_DIM, N_HEADS = (4096, 512, 512, 4)
        D_K = OUT_DIM // N_HEADS
        key = jax.random.key(seed)
        k1, k2, k3, k4, k5 = jax.random.split(key, 5)
        H = jax.random.normal(k1, (N, IN_DIM), dtype=jnp.float32)
        A = jax.random.randint(k2, (N, N), 0, 2, dtype=jnp.int32)
        W = jax.random.normal(k3, (IN_DIM, OUT_DIM), dtype=jnp.float32) * (1.0 / np.sqrt(IN_DIM))
        a_l = jax.random.normal(k4, (N_HEADS, D_K), dtype=jnp.float32) * 0.1
        a_r = jax.random.normal(k5, (N_HEADS, D_K), dtype=jnp.float32) * 0.1
        return {'H': H, 'A': A, 'W': W, 'a_l': a_l, 'a_r': a_r}
    _L2_gnn_all = _L2_gnn_setup()
    _L2_gnn_in = {k: v for k, v in _L2_gnn_all.items() if k in ('W', 'a_l', 'a_r', )}
    del _L2_gnn_all

    def _L3_gnn_setup():
        import jax, jax.numpy as jnp
        import numpy as np
        N = 8192
        D_IN = 512
        D_OUT = 512
        key = jax.random.key(seed)
        k1, k2, k3, k4 = jax.random.split(key, 4)
        node_feats = jax.random.normal(k1, (N, D_IN), dtype=jnp.float32)
        adj_matrix = jax.random.randint(k2, (N, N), 0, 2, dtype=jnp.int32)
        w_self = jax.random.normal(k3, (D_OUT, D_IN), dtype=jnp.float32) * D_IN ** (-0.5)
        w_neigh = jax.random.normal(k4, (D_OUT, D_IN), dtype=jnp.float32) * D_IN ** (-0.5)
        return {'node_feats': node_feats, 'adj_matrix': adj_matrix, 'w_self': w_self, 'w_neigh': w_neigh}
    _L3_gnn_all = _L3_gnn_setup()
    _L3_gnn_in = {k: v for k, v in _L3_gnn_all.items() if k in ('w_self', 'w_neigh', )}
    del _L3_gnn_all

    return {
        "x": x,
        "adj": adj,
        "L0_gnn_W": _L0_gnn_in["W"],
        "L0_gnn_a1": _L0_gnn_in["a1"],
        "L0_gnn_a2": _L0_gnn_in["a2"],
        "L1_gnn_W": _L1_gnn_in["W"],
        "L1_gnn_a": _L1_gnn_in["a"],
        "L2_gnn_W": _L2_gnn_in["W"],
        "L2_gnn_a_l": _L2_gnn_in["a_l"],
        "L2_gnn_a_r": _L2_gnn_in["a_r"],
        "L3_gnn_w_self": _L3_gnn_in["w_self"],
        "L3_gnn_w_neigh": _L3_gnn_in["w_neigh"],
    }

def reference(x, adj, L0_gnn_W, L0_gnn_a1, L0_gnn_a2, L1_gnn_W, L1_gnn_a, L2_gnn_W, L2_gnn_a_l, L2_gnn_a_r, L3_gnn_w_self, L3_gnn_w_neigh):
    import jax
    import jax.numpy as jnp
    def _L0_gnn_ref(x, adj, W, a1, a2):
        import jax, jax.numpy as jnp
        import numpy as np
        N, IN, OUT, H = (4096, 512, 64, 8)
        ALPHA = 0.2
        NEG = -9000000000000000.0

        def glorot(key, shape):
            fan_in, fan_out = (shape[-2], shape[-1])
            limit = np.sqrt(6.0 / (fan_in + fan_out))
            return jax.random.uniform(key, shape, jnp.float32, -limit, limit)
        Wh = jnp.einsum('ni,hio->hno', x, W)
        f1 = jnp.einsum('hno,ho->hn', Wh, a1)
        f2 = jnp.einsum('hno,ho->hn', Wh, a2)
        e = jax.nn.leaky_relu(f1[:, :, None] + f2[:, None, :], ALPHA)
        e = jnp.where(adj[None] > 0, e, NEG)
        attn = jax.nn.softmax(e, axis=-1)
        h = jnp.einsum('hnm,hmo->hno', attn, Wh)
        out = jnp.transpose(h, (1, 0, 2)).reshape(N, H * OUT)
        return out

    def _L1_gnn_ref(h, adj, W, a):
        import jax, jax.numpy as jnp
        import numpy as np
        N, IN, H, D = (4096, 512, 8, 64)
        ALPHA = 0.2
        NEG_BIG = -9000000000000000.0
        n = h.shape[0]
        Wh = (h @ W).reshape(n, H, D)
        a1, a2 = (a[0, :, :D], a[0, :, D:])
        s1 = jnp.einsum('nhd,hd->nh', Wh, a1)
        s2 = jnp.einsum('nhd,hd->nh', Wh, a2)
        e = jax.nn.leaky_relu(s1[:, None, :] + s2[None, :, :], negative_slope=ALPHA)
        att_logits = jnp.where(adj[:, :, None] > 0, e, NEG_BIG)
        attention = jax.nn.softmax(att_logits, axis=1)
        h_prime = jnp.einsum('ijh,jhd->ihd', attention, Wh)
        return jax.nn.elu(h_prime.reshape(n, H * D))

    def _L2_gnn_ref(H, A, W, a_l, a_r):
        import jax, jax.numpy as jnp
        import numpy as np
        NEG_SLOPE = 0.2
        N, IN_DIM, OUT_DIM, N_HEADS = (4096, 512, 512, 4)
        D_K = OUT_DIM // N_HEADS
        n = H.shape[0]
        mask = A + jnp.eye(n, dtype=A.dtype) > 0
        Wh = (H @ W).reshape(n, N_HEADS, D_K)
        sl = jnp.einsum('nhd,hd->nh', Wh, a_l)
        sr = jnp.einsum('nhd,hd->nh', Wh, a_r)
        e = jax.nn.leaky_relu(sl[:, :, None] + sr.T[None, :, :], negative_slope=NEG_SLOPE)
        e = jnp.where(mask[:, None, :], e, -jnp.inf)
        alpha = jnp.nan_to_num(jax.nn.softmax(e, axis=2), nan=0.0)
        out = jnp.einsum('nhm,mhd->nhd', alpha, Wh).reshape(n, OUT_DIM)
        return jax.nn.elu(out)

    def _L3_gnn_ref(node_feats, adj_matrix, w_self, w_neigh):
        import jax, jax.numpy as jnp
        import numpy as np
        N = 8192
        D_IN = 512
        D_OUT = 512
        adj_f = adj_matrix.astype(node_feats.dtype)
        s = adj_f @ node_feats[:, 0]
        has_neigh = jnp.sum(adj_matrix, axis=1) > 0
        s = jnp.where(has_neigh, s, jnp.zeros_like(s))
        neigh_term = s[:, None] * jnp.sum(w_neigh, axis=1)[None, :]
        return jax.nn.relu(node_feats @ w_self.T + neigh_term)

    x = _layernorm(x + _L0_gnn_ref(x, adj, L0_gnn_W, L0_gnn_a1, L0_gnn_a2), axis=-1)
    x = _layernorm(x + _L1_gnn_ref(x, adj, L1_gnn_W, L1_gnn_a), axis=-1)
    x = _layernorm(x + _L2_gnn_ref(x, adj, L2_gnn_W, L2_gnn_a_l, L2_gnn_a_r), axis=-1)
    x = _layernorm(x + _L3_gnn_ref(x, adj, L3_gnn_w_self, L3_gnn_w_neigh), axis=-1)
    return x


_drawn_inputs = setup_inputs


def setup_inputs(seed=0):
    import zlib

    import numpy as np

    out = dict(_drawn_inputs(seed))
    spreads = {}
    factors = {'L2_gnn_a_l': 3.69}
    for name, (base, spread) in spreads.items():
        noise = np.random.default_rng([zlib.crc32(name.encode()), seed]).standard_normal(out[name].shape)
        drawn = base * np.exp(spread * noise) if base else spread * noise
        out[name] = jnp.asarray(drawn.astype(out[name].dtype))
    for name, factor in factors.items():
        out[name] = (out[name] * factor).astype(out[name].dtype)
    return out
```

```python
import concourse.bass as bass
from concourse import mybir
from contextlib import ExitStack

F32 = mybir.dt.float32
BF16 = mybir.dt.bfloat16
F16 = mybir.dt.float16
I8 = mybir.dt.int8
I32 = mybir.dt.int32
ALU = mybir.AluOpType
ACT = mybir.ActivationFunctionType
AX = mybir.AxisListType

N = 4096
F = 512
P = 128
NC = N // P
KC = F // P
EPS = 1e-5
SLOPE = 0.2
VSCALE = 512.0
IB = 1024
NIB = N // IB
CB = IB // P
PASSES = 4


ONE = 1


def start_at_one(nc, sems):
    for s in sems:
        nc.gpsimd.sem_inc(s, ONE)
    nc.all_engine_barrier()


def free_semaphores(nc, sems):
    nc.clear_and_free_semaphores(sems)
    nc.all_engine_barrier()


class Layer:

    def __init__(self, heads):
        self.H = heads
        self.D = F // heads
        self.HP = heads // PASSES
        self.VW = 2 * 2 * (self.D + 1)


def load_adjacency(nc, adj, code, ident_bf):
    ctx = ExitStack()
    with ctx:
        raw = [ctx.enter_context(nc.sbuf_tensor(f"adj_raw{b}", [P, N], I32)) for b in range(2)]
        one = [ctx.enter_context(nc.sbuf_tensor(f"adj_one{b}", [P, N], BF16)) for b in range(2)]
        turned = [[ctx.enter_context(nc.psum_tensor(f"adj_turned{b}{g}", [P, 8, P], BF16)) for g in range(4)]
                  for b in range(2)]

        sems = []

        def sem(name):
            sems.append(nc.alloc_semaphore(name))
            return sems[-1]

        loaded = [sem(f"adj_loaded{b}") for b in range(2)]
        converted = [sem(f"adj_converted{b}") for b in range(2)]
        bank_turned = [sem(f"adj_bank_turned{b}") for b in range(2)]
        coded_dve = [sem(f"adj_coded_dve{b}") for b in range(2)]
        coded_act = [sem(f"adj_coded_act{b}") for b in range(2)]
        start_at_one(nc, sems)
        block = ctx.enter_context(nc.Block())

        @block.sync
        def _(sp):
            with sp.Fori(0, NC // 2) as t:
                for b in range(2):
                    sp.wait_ge(converted[b], ONE + t)
                    sp.dma_start(raw[b][:, :], adj[bass.ds((2 * t + b) * P, P), :]).then_inc(loaded[b], 16)

        @block.vector
        def _(dve):
            with dve.Fori(0, NC // 2) as t:
                for b in range(2):
                    dve.wait_ge(loaded[b], ONE + 16 * t + 16)
                    dve.wait_ge(bank_turned[b], ONE + 4 * t)
                    nc.vector.tensor_scalar(one[b][:, :], raw[b][:, :], 0.0, None, ALU.is_gt)\
                        .then_inc(converted[b], 1)
                    for g in range(2):
                        dve.wait_ge(bank_turned[b], ONE + 4 * t + g + 1)
                        nc.vector.tensor_scalar(code[:, 8 * g:8 * g + 8, bass.ds((2 * t + b) * P, P)],
                                                turned[b][g][:, :, :], 2.0, -1.0, ALU.mult, ALU.add)\
                            .then_inc(coded_dve[b], 1)

        @block.scalar
        def _(act):
            with act.Fori(0, NC // 2) as t:
                for b in range(2):
                    for g in range(2, 4):
                        act.wait_ge(bank_turned[b], ONE + 4 * t + g + 1)
                        nc.scalar.activation(code[:, 8 * g:8 * g + 8, bass.ds((2 * t + b) * P, P)],
                                             turned[b][g][:, :, :], ACT.Copy, bias=-1.0, scale=2.0)\
                            .then_inc(coded_act[b], 1)

        @block.tensor
        def _(pe):
            with pe.Fori(0, NC // 2) as t:
                for b in range(2):
                    pe.wait_ge(converted[b], ONE + t + 1)
                    pe.wait_ge(coded_dve[b], ONE + 2 * t)
                    pe.wait_ge(coded_act[b], ONE + 2 * t)
                    for g in range(4):
                        for c in range(8):
                            j = (8 * g + c) * P
                            last = nc.tensor.transpose(turned[b][g][:, c, :], one[b][:, j:j + P], ident_bf[:, :])
                        last.then_inc(bank_turned[b], 1)
    free_semaphores(nc, sems)


class Norm:

    def __init__(self, nc, sb, sem, G):
        self.nc, self.G = nc, G
        self.stats = sb("stats", [P, G, 6], F32)
        self.mt = sb("mt", [P, 5, G], F32)
        self.mean = sb("mean", [P, G], F32)
        self.ve = sb("ve", [P, G], F32)
        self.lnv = sb("lnv", [P, G], F32)
        self.rs0 = sb("rs0", [P, G], F32)
        self.rt = sb("rt", [P, 3, G], F32)
        self.rs = sb("rs", [P, G], F32)
        self.step = sem("norm_step")
        self.STEPS = G + 10
        self.ve_ready, self.ln_done, self.rs0_ready = sem("ve_ready"), sem("ln_done"), sem("rs0_ready")
        self.ready = sem("x_ready")

    def rows(self, dve, g, x, b):
        nc, G, step, base = self.nc, self.G, self.step, ONE + self.STEPS * g
        st, mt = self.stats, self.mt
        for c in range(G):
            nc.vector.bn_stats(st[:, c, :], x[:, b, c, :]).then_inc(step, 1)
        dve.wait_ge(self.ready, ONE + G * g)
        dve.wait_ge(step, base + G)
        nc.vector.tensor_tensor(mt[:, 0, :], st[:, :, 1], st[:, :, 4], ALU.subtract).then_inc(step, 1)
        nc.vector.tensor_tensor(mt[:, 1, :], st[:, :, 1], st[:, :, 4], ALU.add).then_inc(step, 1)
        nc.vector.tensor_tensor(mt[:, 2, :], st[:, :, 2], st[:, :, 5], ALU.add).then_inc(step, 1)
        dve.wait_ge(step, base + G + 3)
        nc.vector.tensor_tensor(mt[:, 3, :], mt[:, 0, :], mt[:, 0, :], ALU.mult).then_inc(step, 1)
        nc.vector.tensor_scalar(mt[:, 4, :], mt[:, 2, :], 1.0 / F, EPS, ALU.mult, ALU.add).then_inc(step, 1)
        nc.vector.tensor_scalar(self.mean[:, :], mt[:, 1, :], 0.5, None, ALU.mult).then_inc(step, 1)
        dve.wait_ge(step, base + G + 6)
        nc.vector.scalar_tensor_tensor(self.ve[:, :], mt[:, 3, :], 0.25, mt[:, 4, :], ALU.mult, ALU.add).then_inc(self.ve_ready, 1)
        dve.wait_ge(self.rs0_ready, ONE + g + 1)
        nc.vector.tensor_tensor(self.rt[:, 0, :], self.rs0[:, :], self.rs0[:, :], ALU.mult).then_inc(step, 1)
        dve.wait_ge(step, base + G + 6 + 1)
        nc.vector.tensor_tensor(self.rt[:, 1, :], self.rt[:, 0, :], self.ve[:, :], ALU.mult).then_inc(step, 1)
        dve.wait_ge(step, base + G + 6 + 2)
        nc.vector.tensor_scalar(self.rt[:, 2, :], self.rt[:, 1, :], -0.5, 1.5, ALU.mult, ALU.add).then_inc(step, 1)
        dve.wait_ge(step, base + G + 6 + 3)
        nc.vector.tensor_tensor(self.rs[:, :], self.rt[:, 2, :], self.rs0[:, :], ALU.mult).then_inc(step, 1)
        dve.wait_ge(step, base + G + 6 + 4)
        for c in range(G):
            nc.vector.tensor_scalar(x[:, b, c, :], x[:, b, c, :], self.mean[:, c:c + 1], self.rs[:, c:c + 1],
                                    ALU.subtract, ALU.mult).then_inc(self.ready, 1)

    def rsqrt(self, act, g):
        act.wait_ge(self.ve_ready, ONE + g + 1)
        self.nc.scalar.activation(self.lnv[:, :], self.ve[:, :], ACT.Ln).then_inc(self.ln_done, 1)
        act.wait_ge(self.ln_done, ONE + g + 1)
        self.nc.scalar.activation(self.rs0[:, :], self.lnv[:, :], ACT.Exp, scale=-0.5).then_inc(self.rs0_ready, 1)


def add_elu(nc, dve, g, xg, og, neg, sems):
    dve.wait_ge(sems["added"], ONE + 2 * g)
    nc.vector.tensor_scalar(neg[:, :, :], og, 0.0, None, ALU.min).then_inc(sems["neg"], 1)
    nc.vector.scalar_tensor_tensor(xg, og, 0.0, xg, ALU.max, ALU.add).then_inc(sems["added"], 1)
    dve.wait_ge(sems["exp"], ONE + g + 1)
    dve.wait_ge(sems["added"], ONE + 2 * g + 1)
    nc.vector.scalar_tensor_tensor(xg, neg[:, :, :], -1.0, xg, ALU.add, ALU.add).then_inc(sems["added"], 1)


def prepare(nc, lay, number, x_in, attn, elu, w, a_src, a_dst, x_out, v_dram, f1_dram, cols, ident):
    H, D = lay.H, lay.D
    f12, beta, rowf = cols
    G = 4
    NG = NC // G
    ln = attn is not None
    LOADS = 16 * (2 if ln else 1)
    ctx = ExitStack()
    with ctx:
        def sb(name, shape, dt):
            return ctx.enter_context(nc.sbuf_tensor(f"{name}_{number}", shape, dt))

        def ps(name, shape, dt):
            return ctx.enter_context(nc.psum_tensor(f"{name}_{number}", shape, dt))

        sems = []

        def sem(name):
            sems.append(nc.alloc_semaphore(f"{name}_{number}"))
            return sems[-1]

        w_sb = sb("w_sb", [P, KC, F], F32)
        wa_tmp = sb("wa_tmp", [P, KC, F], F32)
        a_bc = sb("a_bc", [P, 2, F], F32)
        wa = sb("wa", [P, KC, 2 * H], F32)
        x = sb("x", [P, 2, G, F], F32)
        if ln:
            o = sb("o", [P, 2, G, F], F32)
            neg = wa_tmp
            norm = Norm(nc, sb, sem, G)
            eluw = {k: sem(f"elu_{k}") for k in ("neg", "exp", "added")}
            x_ready = norm.ready
        xT = sb("xT", [P, G, KC, P], F32)
        fst = sb("fst", [P, G, 2 * H], F32)
        fT = sb("fT", [2 * H, G, P], F32)
        ebd = sb("ebd", [P, G, 2, H], F32)
        ebr = sb("ebr", [P, G, 2, H], BF16)
        rec = sb("rec", [P, G, 2, H], F32)
        rho = sb("rho", [P, G, 2, H], F32)
        vf = [sb(f"vf{b}", [P, H, 2, D + 1], F32) for b in range(2)]
        vh = [sb(f"vh{b}", [P, H, 2, 2, D + 1], F16) for b in range(2)]
        rfm = sb("rfm", [P, NC, H, 2], F32)
        pT = [ps(f"pT{b}", [P, KC, P], F32) for b in range(2)]
        pW = [ps(f"pW{b}", [P, F], F32) for b in range(2)]
        pF = ps("pF", [P, G, P], F32)[:, :, 0:2 * H]
        pFT = ps("pFT", [P, G, P], F32)[0:2 * H, :, :]

        w_loaded, a_loaded = sem("w_loaded"), sem("a_loaded")
        wa_step, wa_ready = sem("wa_step"), sem("wa_ready")
        x_loaded = [sem(f"x_loaded{b}") for b in range(2)]
        x_stored = [sem(f"x_stored{b}") for b in range(2)]
        turned = [sem(f"turned{b}") for b in range(2)]
        xT_ready = sem("xT_ready")
        f_done, f_copied = sem("f_done"), sem("f_copied")
        fT_done, fT_copied, fT_stored = sem("fT_done"), sem("fT_copied"), sem("fT_stored")
        wx_done, rho_step, v_ready = sem("wx_done"), sem("rho_step"), sem("v_ready")
        high_ready, low_ready = sem("high_ready"), sem("low_ready")
        v_stored = [sem(f"v_stored{b}") for b in range(2)]
        rf_step, rf_ready = sem("rf_step"), sem("rf_ready")
        start_at_one(nc, sems)
        block = ctx.enter_context(nc.Block())

        x_v = x_in.rearrange("(g c p) f -> g p c f", c=G, p=P)
        o_v = attn.rearrange("(g c p) f -> g p c f", c=G, p=P) if ln else None
        xo_v = x_out.rearrange("(g c p) f -> g p c f", c=G, p=P) if ln else None
        f1_v = f1_dram[0:H, :].rearrange("h (g c p) -> g h c p", c=G, p=P)
        v_v = v_dram[:, 0:H * lay.VW].rearrange("(c p) m -> c p m", p=P)

        @block.sync
        def _(sp):
            for kc in range(KC):
                dst = w_sb[:, kc, :]
                sp.dma_start(dst if len(w[kc].shape) == 2 else dst.rearrange("p (h o) -> p h o", h=H), w[kc])\
                    .then_inc(w_loaded, 16)
            for k, a in enumerate((a_src, a_dst)):
                dst = a_bc[:, k, :] if len(a.shape) == 1 else a_bc[:, k, :].rearrange("p (h o) -> p h o", h=H)
                sp.dma_start(dst, a.partition_broadcast(P)).then_inc(a_loaded, 16)
            with sp.Fori(0, NG // 2) as r:
                for b in range(2):
                    sp.wait_ge(turned[b], ONE + G * r)
                    if ln:
                        sp.wait_ge(x_stored[b], ONE + 16 * r)
                    sp.dma_start(x[:, b, :, :], x_v[2 * r + b]).then_inc(x_loaded[b], 16)
                    if ln:
                        sp.dma_start(o[:, b, :, :], o_v[2 * r + b]).then_inc(x_loaded[b], 16)

        @block.vector
        def _(dve):
            dve.wait_ge(w_loaded, ONE + 16 * KC)
            dve.wait_ge(a_loaded, ONE + 32)
            for k in range(2):
                nc.vector.tensor_tensor(wa_tmp[:, :, :], w_sb[:, :, :],
                                        a_bc[:, k:k + 1, :].to_broadcast([P, KC, F]), ALU.mult).then_inc(wa_step, 1)
                dve.wait_ge(wa_step, ONE + 2 * k + 1)
                nc.vector.tensor_reduce(wa[:, :, k * H:(k + 1) * H],
                                        wa_tmp[:, :, :].rearrange("p k (h o) -> p k h o", h=H), AX.X, ALU.add)\
                    .then_inc(wa_step, 1)
                dve.wait_ge(wa_step, ONE + 2 * k + 2)

            def layernorm(g, r, b):
                dve.wait_ge(x_loaded[b], ONE + LOADS * r + LOADS)
                xg, og = x[:, b, :, :], o[:, b, :, :]
                if elu:
                    add_elu(nc, dve, g, xg, og, neg, eluw)
                else:
                    nc.vector.tensor_tensor(xg, og, xg, ALU.add).then_inc(eluw["added"], 2)
                dve.wait_ge(eluw["added"], ONE + 2 * g + 2)
                norm.rows(dve, g, x, b)

            def values(g):
                dve.wait_ge(f_copied, ONE + 4 * g + 4)
                nc.vector.tensor_copy(ebr[:, :, :, :], ebd[:, :, :, :]).then_inc(rho_step, 1)
                dve.wait_ge(rho_step, ONE + 4 * g + 1)
                nc.vector.reciprocal(rec[:, :, :, :], ebr[:, :, :, :]).then_inc(rho_step, 1)
                nc.vector.tensor_copy(beta[:, bass.ds(G * g, G), :, 0:H], ebr[:, :, :, :]).then_inc(rho_step, 1)
                dve.wait_ge(rho_step, ONE + 4 * g + 3)
                nc.vector.scalar_tensor_tensor(rho[:, :, :, :], ebd[:, :, :, :], VSCALE, rec[:, :, :, :],
                                               ALU.mult, ALU.mult).then_inc(rho_step, 1)
                dve.wait_ge(rho_step, ONE + 4 * g + 4)
                for c in range(G):
                    b = c % 2
                    if c >= 2:
                        dve.wait_ge(high_ready, ONE + G * g + c - 1)
                        dve.wait_ge(low_ready, ONE + G * g + c - 1)
                    else:
                        dve.wait_ge(low_ready, ONE + G * g)
                        dve.wait_ge(high_ready, ONE + G * g)
                    nc.vector.tensor_copy(vf[b][:, :, :, D:D + 1],
                                          rho[:, c, :, :].rearrange("p k (h o) -> p h k o", o=1)).then_inc(v_ready, 1)
                    dve.wait_ge(wx_done, ONE + G * g + c + 1)
                    for k in range(2):
                        nc.vector.tensor_tensor(vf[b][:, :, k, 0:D], pW[b][:, :].rearrange("p (h o) -> p h o", h=H),
                                                rho[:, c, k, :].rearrange("p (h o) -> p h o", o=1).to_broadcast([P, H, D]), ALU.mult)\
                            .then_inc(v_ready, 1)

            if ln:
                layernorm(0, 0, 0)
                with dve.Fori(0, NG // 2 - 1) as r:
                    layernorm(2 * r + 1, r, 1)
                    values(2 * r)
                    layernorm(2 * r + 2, r + 1, 0)
                    values(2 * r + 1)
                layernorm(NG - 1, NG // 2 - 1, 1)
                values(NG - 2)
                values(NG - 1)
            else:
                with dve.Fori(0, NG) as g:
                    values(g)
            f1 = f12[:, :, 0:H]
            for k, s in enumerate((1.0 - SLOPE, SLOPE - 1.0)):
                nc.vector.tensor_scalar(rfm[:, :, :, k], f1, s, 0.0, ALU.mult, ALU.min).then_inc(rf_step, 1)

        @block.scalar
        def _(act):
            def rsqrt(g):
                if elu:
                    act.wait_ge(eluw["neg"], ONE + g + 1)
                    nc.scalar.activation(neg[:, :, :], neg[:, :, :], ACT.Exp).then_inc(eluw["exp"], 1)
                norm.rsqrt(act, g)

            def turn(g, r, b):
                act.wait_ge(wx_done, ONE + G * g)
                for c in range(G):
                    act.wait_ge(turned[b], ONE + G * r + c + 1)
                    nc.scalar.activation(xT[:, c, :, :], pT[c % 2][:, :, :], ACT.Copy).then_inc(xT_ready, 1)
                act.wait_ge(f_done, ONE + g + 1)
                act.wait_ge(fT_done, ONE + g)
                nc.scalar.activation(fst[:, :, :], pF, ACT.Copy).then_inc(f_copied, 1)
                nc.scalar.activation(f12[:, bass.ds(G * g, G), 0:2 * H], pF, ACT.Copy).then_inc(f_copied, 1)
                act.wait_ge(rho_step, ONE + 4 * g)
                nc.scalar.activation(ebd[:, :, 0, :], pF[:, :, H:2 * H], ACT.Exp).then_inc(f_copied, 1)
                nc.scalar.activation(ebd[:, :, 1, :], pF[:, :, H:2 * H], ACT.Exp, scale=SLOPE).then_inc(f_copied, 1)
                act.wait_ge(fT_done, ONE + g + 1)
                act.wait_ge(fT_stored, ONE + 16 * g)
                nc.scalar.activation(fT[:, :, :], pFT, ACT.Copy).then_inc(fT_copied, 1)
                act.wait_ge(fT_copied, ONE + g + 1)
                act.dma_start(f1_v[g], fT[0:H, :, :]).then_inc(fT_stored, 16)

            def high(g):
                def store(c):
                    act.wait_ge(low_ready, ONE + G * g + c + 1)
                    act.dma_start(v_v[G * g + c], vh[c % 2][:, :, :, :, :].rearrange("p h k s d -> p (h k s d)"))\
                        .then_inc(v_stored[c % 2], 16)

                for c in range(G):
                    b = c % 2
                    act.wait_ge(v_stored[b], ONE + 16 * (2 * g + c // 2))
                    act.wait_ge(v_ready, ONE + 3 * (G * g + c) + 3)
                    nc.scalar.activation(vh[b][:, :, :, 0, :], vf[b][:, :, :, :], ACT.Copy).then_inc(high_ready, 1)
                    if c:
                        store(c - 1)
                store(G - 1)

            def store_rows(g, r, b):
                act.wait_ge(x_ready, ONE + G * (g + 1))
                act.dma_start(xo_v[g], x[:, b, :, :]).then_inc(x_stored[b], 16)

            def rows(g, r, b):
                if ln:
                    rsqrt(g)
                    store_rows(g, r, b)

            rows(0, 0, 0)
            turn(0, 0, 0)
            with act.Fori(0, NG // 2 - 1) as r:
                rows(2 * r + 1, r, 1)
                high(2 * r)
                turn(2 * r + 1, r, 1)
                rows(2 * r + 2, r + 1, 0)
                high(2 * r + 1)
                turn(2 * r + 2, r + 1, 0)
            rows(NG - 1, NG // 2 - 1, 1)
            high(NG - 2)
            turn(NG - 1, NG // 2 - 1, 1)
            high(NG - 1)
            if ln:
                for b in range(2):
                    act.wait_ge(x_stored[b], ONE + 16 * (NG // 2))
            act.wait_ge(fT_stored, ONE + 16 * NG)
            for b in range(2):
                act.wait_ge(v_stored[b], ONE + 16 * (NC // 2))
            act.wait_ge(rf_step, ONE + 2)
            nc.scalar.activation(rowf[:, :, 0:2 * H], rfm[:, :, :, :].rearrange("p c h k -> p c (h k)"), ACT.Exp).then_inc(rf_ready, 1)

        @block.gpsimd
        def _(pool):
            with pool.Fori(0, NC // 2) as t:
                for b in range(2):
                    pool.wait_ge(high_ready, ONE + 2 * t + b + 1)
                    nc.gpsimd.tensor_tensor(vh[b][:, :, :, 1, :], vf[b][:, :, :, :], vh[b][:, :, :, 0, :], ALU.subtract)\
                        .then_inc(low_ready, 1)

        @block.tensor
        def _(pe):
            def group(g, r, b):
                for c in range(G):
                    if ln:
                        pe.wait_ge(x_ready, ONE + G * g + c + 1)
                    elif c == 0:
                        pe.wait_ge(x_loaded[b], ONE + LOADS * r + LOADS)
                    if c < 2:
                        pe.wait_ge(xT_ready, ONE + G * g)
                    else:
                        pe.wait_ge(xT_ready, ONE + G * g + c - 1)
                    for kc in range(KC):
                        last = nc.tensor.transpose(pT[c % 2][:, kc, :], x[:, b, c, kc * P:(kc + 1) * P], ident[:, :])
                    last.then_inc(turned[b], 1)
                pe.wait_ge(f_copied, ONE + 4 * g)
                for c in range(G):
                    pe.wait_ge(xT_ready, ONE + G * g + c + 1)
                    for kc in range(KC):
                        last = nc.tensor.matmul(pF[:, c, :], xT[:, c, kc, :], wa[:, kc, :], start=kc == 0, stop=kc == KC - 1)
                last.then_inc(f_done, 1)
                pe.wait_ge(f_copied, ONE + 4 * g + 1)
                pe.wait_ge(fT_copied, ONE + g)
                for c in range(G):
                    last = nc.tensor.transpose(pFT[:, c, :], fst[:, c, :], ident[:, :])
                last.then_inc(fT_done, 1)
                for c in range(G):
                    if c < 2:
                        pe.wait_ge(v_ready, ONE + 3 * G * g)
                    else:
                        pe.wait_ge(v_ready, ONE + 3 * (G * g + c - 1))
                    for kc in range(KC):
                        last = nc.tensor.matmul(pW[c % 2][:, :], xT[:, c, kc, :], w_sb[:, kc, :],
                                                start=kc == 0, stop=kc == KC - 1)
                    last.then_inc(wx_done, 1)

            pe.wait_ge(wa_step, ONE + 4)
            with pe.Fori(0, NG // 2) as r:
                for b in range(2):
                    group(2 * r + b, r, b)
    free_semaphores(nc, sems)


def attend(nc, lay, number, code, v_dram, f1_dram, attn, cols, ident_bf):
    H, D, HP, VW = lay.H, lay.D, lay.HP, lay.VW
    f12, beta, rowf = cols
    D1 = D + 1
    PW = HP * VW
    BLOCKS = PASSES * NIB
    PAIRS = NC // 2
    VL = 8
    ctx = ExitStack()
    with ctx:
        def sb(name, shape, dt):
            return ctx.enter_context(nc.sbuf_tensor(f"{name}_{number}", shape, dt))

        sems = []

        def sem(name):
            sems.append(nc.alloc_semaphore(f"{name}_{number}"))
            return sems[-1]

        val = sb("val", [P, NC, PW], F16)
        f1b = [sb(f"f1b{b}", [P, HP, IB], F32) for b in range(2)]
        mask = [sb(f"mask{b}", [P, IB], BF16) for b in range(2)]
        y = [sb(f"y{b}", [P, HP, IB], BF16) for b in range(2)]
        S = [sb(f"S{b}", [P, HP, IB], BF16) for b in range(2)]
        T = [sb(f"T{b}", [P, HP, IB], BF16) for b in range(2)]
        part = sb("part", [P, 2, CB, HP, D1], F32)
        rden = sb("rden", [P, CB, HP], F32)
        res = part[:, 1, :, :, :].rearrange("p c h d -> p (c h d)")[:, 0:CB * HP * D]\
            .rearrange("p (c h d) -> p c h d", c=CB, h=HP)
        acc = ctx.enter_context(nc.psum_tensor(f"acc_{number}", [P, CB, 512], F32))

        v_loaded = sem("val_loaded")
        f1_loaded = [sem(f"f1_loaded{b}") for b in range(2)]
        f1_used = [sem(f"f1_used{b}") for b in range(2)]
        mask_loaded = [nc.alloc_semaphore(f"mask_loaded{b}_{number}") for b in range(2)]
        from_zero = list(mask_loaded)
        y_ready = [sem(f"y_ready{b}") for b in range(2)]
        z_ready = [sem(f"z_ready{b}") for b in range(2)]
        st_ready = [sem(f"st_ready{b}") for b in range(2)]
        st_used = [sem(f"st_used{b}") for b in range(2)]
        acc_read, sum_step, res_ready, res_stored = sem("acc_read"), sem("sum_step"), sem("res_ready"), sem("res_stored")
        start_at_one(nc, sems)
        block = ctx.enter_context(nc.Block())

        v_v = v_dram.rearrange("(q c p) m -> q p c m", c=NC // VL, p=P)
        out_v = attn.rearrange("(b c p) f -> b p c f", c=CB, p=P)

        @block.sync
        def _(sp):
            def f1_load(m, b):
                sp.dma_start(f1b[b][:, :, :],
                             f1_dram[bass.ds(m // NIB * HP, HP), bass.ds(m % NIB * IB, IB)].partition_broadcast(P))\
                    .then_inc(f1_loaded[b], 16)

            def v_load(p, q):
                sp.dma_start(val[:, q * (NC // VL):(q + 1) * (NC // VL), :], v_v[q][:, :, bass.ds(p * PW, PW)])\
                    .then_inc(v_loaded, 16)

            def store(m):
                sp.wait_ge(res_ready, ONE + m + 1)
                sp.dma_start(out_v[m % NIB][:, :, bass.ds(m // NIB * P, P)],
                             res.rearrange("p c h d -> p c (h d)")).then_inc(res_stored, 16)

            f1_load(0, 0)
            for q in range(VL):
                v_load(0, q)
            f1_load(1, 1)
            with sp.Fori(0, PASSES - 1) as p:
                for ib in range(NIB):
                    m = p * NIB + ib
                    if ib == NIB - 1:
                        for q in range(VL):
                            for b in range(2):
                                sp.wait_ge(st_used[b], ONE + PAIRS * m + (q + 1) * PAIRS // VL)
                            v_load(p + 1, q)
                    sp.wait_ge(f1_used[ib % 2], ONE + p * (NIB // 2) + ib // 2 + 1)
                    f1_load(m + 2, ib % 2)
                    store(m)
            for ib in range(NIB):
                m = (PASSES - 1) * NIB + ib
                if ib < NIB - 2:
                    sp.wait_ge(f1_used[ib % 2], ONE + (PASSES - 1) * (NIB // 2) + ib // 2 + 1)
                    f1_load(m + 2, ib % 2)
                store(m)
            sp.wait_ge(res_stored, ONE + 16 * BLOCKS)

        @block.gpsimd
        def _(pool):
            with pool.Fori(0, PASSES) as p:
                with pool.Fori(0, NIB) as ib:
                    with pool.Fori(0, PAIRS) as jj:
                        for b in range(2):
                            r = (p * NIB + ib) * PAIRS + jj
                            pool.wait_ge(z_ready[b], ONE + HP * r)
                            pool.dma_start(mask[b][:, :], code[:, 2 * jj + b, bass.ds(ib * IB, IB)])\
                                .then_inc(mask_loaded[b], 16)

        @block.scalar
        def _(act):
            with act.Fori(0, PASSES) as p:
                with act.Fori(0, NIB // 2) as i2:
                    for s in range(2):
                        act.wait_ge(f1_loaded[s], ONE + 16 * (p * (NIB // 2) + i2) + 16)
                        with act.Fori(0, PAIRS) as jj:
                            for b in range(2):
                                r = (p * NIB + 2 * i2 + s) * PAIRS + jj
                                act.wait_ge(st_ready[b], ONE + 2 * HP * r)
                                for h in range(HP):
                                    nc.scalar.activation(y[b][:, h, :], f1b[s][:, h, :], ACT.Relu,
                                                         bias=f12[:, 2 * jj + b, bass.ds(H + p * HP + h, 1)])\
                                        .then_inc(y_ready[b], 1)
                        for b in range(2):
                            act.wait_ge(y_ready[b], ONE + HP * PAIRS * (p * NIB + 2 * i2 + s + 1))
                        act.sem_inc(f1_used[s], 1)

        @block.vector
        def _(dve):
            def pair(m, jj):
                p = m // NIB
                for b in range(2):
                    r = m * PAIRS + jj
                    dve.wait_ge(mask_loaded[b], 16 * r + 16)
                    for h in range(HP):
                        dve.wait_ge(y_ready[b], ONE + HP * r + h + 1)
                        nc.vector.tensor_tensor(y[b][:, h, :], y[b][:, h, :], mask[b][:, :], ALU.min)\
                            .then_inc(z_ready[b], 1)
                    dve.wait_ge(st_used[b], ONE + r)
                    for h in range(HP):
                        dve.wait_ge(z_ready[b], ONE + HP * r + h + 1)
                        for k, (M, op) in enumerate(((S, ALU.is_gt), (T, ALU.is_equal))):
                            nc.vector.tensor_scalar(M[b][:, h, :], y[b][:, h, :], 0.0,
                                                    beta[:, 2 * jj + b, k, bass.ds(p * HP + h, 1)], op, ALU.mult)\
                                .then_inc(st_ready[b], 1)

            def normalise(m):
                p, ib = m // NIB, m % NIB
                for b in range(2):
                    dve.wait_ge(st_used[b], ONE + PAIRS * m + PAIRS)
                dve.wait_ge(sum_step, ONE + 2 * m)
                dve.wait_ge(res_stored, ONE + 16 * m)
                for k in range(2):
                    nc.vector.tensor_tensor(part[:, k, :, :, :],
                                            acc[:, :, 0:2 * HP * D1].rearrange("p c (h k d) -> p k c h d", k=2, d=D1)[:, k],
                                            rowf[:, bass.ds(ib * CB, CB), bass.ds(p * 2 * HP, 2 * HP)]
                                            .rearrange("p c (h k o) -> p k c h o", k=2, o=1)[:, k]
                                            .to_broadcast([P, CB, HP, D1]), ALU.mult).then_inc(acc_read, 1)
                dve.wait_ge(acc_read, ONE + 2 * m + 2)
                nc.vector.tensor_tensor(part[:, 0, :, :, :], part[:, 0, :, :, :], part[:, 1, :, :, :], ALU.add)\
                    .then_inc(sum_step, 1)
                dve.wait_ge(sum_step, ONE + 2 * m + 1)
                nc.vector.reciprocal(rden[:, :, :], part[:, 0, :, :, D]).then_inc(sum_step, 1)
                dve.wait_ge(sum_step, ONE + 2 * m + 2)
                nc.vector.tensor_tensor(res, part[:, 0, :, :, 0:D],
                                        rden[:, :, :].rearrange("p c (h o) -> p c h o", o=1).to_broadcast([P, CB, HP, D]),
                                        ALU.mult).then_inc(res_ready, 1)

            pair(0, 0)
            with dve.Fori(0, BLOCKS - 1) as m:
                with dve.Fori(1, PAIRS) as jj:
                    pair(m, jj)
                pair(m + 1, 0)
                normalise(m)
            with dve.Fori(1, PAIRS) as jj:
                pair(BLOCKS - 1, jj)
            normalise(BLOCKS - 1)

        @block.tensor
        def _(pe):
            with pe.Fori(0, BLOCKS) as m:
                pe.wait_ge(acc_read, ONE + 2 * m)
                pe.wait_ge(v_loaded, ONE + 16 * VL * (m // NIB + 1))
                for c in range(CB):
                    nc.tensor.matmul(acc[:, c, 510:512], ident_bf[:, :], ident_bf[:, 0:2], start=True, stop=True,
                                     skip_group_check=True)
                with pe.Fori(0, PAIRS) as jj:
                    for b in range(2):
                        r = m * PAIRS + jj
                        for h in range(HP):
                            for k, M in enumerate((S, T)):
                                pe.wait_ge(st_ready[b], ONE + 2 * HP * r + 2 * h + k + 1)
                                for c in range(CB):
                                    at = (2 * h + k) * D1
                                    for part_of in range(2):
                                        v0 = (2 * (2 * h + k) + part_of) * D1
                                        last = nc.tensor.matmul(acc[:, c, at:at + D1], M[b][:, h, c * P:(c + 1) * P],
                                                                val[:, 2 * jj + b, v0:v0 + D1], start=False, stop=False,
                                                                skip_group_check=True)
                        last.then_inc(st_used[b], 1)
    free_semaphores(nc, sems + from_zero)


def last_layer(nc, x_in, attn, w_self, w_neigh, code, y_dram, x_dram, out, ident, ident_bf):
    number = 3
    G = 4
    NG = NC // G
    ctx = ExitStack()
    with ctx:
        def sb(name, shape, dt):
            return ctx.enter_context(nc.sbuf_tensor(f"{name}_{number}", shape, dt))

        r_bc = sb("r_bc", [P, F], F32)
        x0 = sb("x0", [P, NC], F32)
        s_col = sb("s_col", [P, NC], F32)
        self_product(nc, G, NG, x_in, attn, w_self, w_neigh, y_dram, x_dram, ident, r_bc, x0)
        neighbour_sums(nc, code, ident_bf, x0, s_col)
        combine(nc, G, NG, y_dram, x_dram, r_bc, s_col, out)


def self_product(nc, G, NG, x_in, attn, w_self, w_neigh, y_dram, x_dram, ident, r_bc, x0):
    ctx = ExitStack()
    with ctx:
        def sb(name, shape, dt):
            return ctx.enter_context(nc.sbuf_tensor(f"{name}_3a", shape, dt))

        def ps(name, shape, dt):
            return ctx.enter_context(nc.psum_tensor(f"{name}_3a", shape, dt))

        sems = []

        def sem(name):
            sems.append(nc.alloc_semaphore(f"{name}_3a"))
            return sems[-1]

        w_rows = sb("w_rows", [P, 2, KC, F], F32)
        wT = sb("wT", [P, KC, F], F32)
        rn = sb("rn", [P, KC], F32)
        rn_b = sb("rn_b", [P, KC, P], F32)
        x = sb("x", [P, 2, G, F], F32)
        o = sb("o", [P, 2, G, F], F32)
        neg = sb("neg", [P, G, F], F32)
        xT = sb("xT", [P, 2, KC, P], F32)
        ys = sb("ys", [P, 2, F], F32)
        norm = Norm(nc, sb, sem, G)
        eluw = {k: sem(f"elu_{k}") for k in ("neg", "exp", "added")}
        pT = [ps(f"pT{b}", [P, KC, P], F32) for b in range(2)]
        pW = [ps(f"pW{b}", [P, F], F32) for b in range(2)]
        w_loaded, rn_ready, rnb_ready, r_done, r_copied = (sem(n) for n in ("w_loaded", "rn_ready", "rnb_ready", "r_done", "r_copied"))
        w_turned, wT_ready = sem("w_turned"), sem("wT_ready")
        x_loaded = [sem(f"x_loaded{b}") for b in range(2)]
        x_stored = [sem(f"x_stored{b}") for b in range(2)]
        x0_ready = sem("x0_ready")
        turned = [sem(f"turned{b}") for b in range(2)]
        xT_ready, y_done, y_copied = sem("xT_ready"), sem("y_done"), sem("y_copied")
        y_stored = [sem(f"y_stored{b}") for b in range(2)]
        start_at_one(nc, sems)
        block = ctx.enter_context(nc.Block())
        x_v = x_in.rearrange("(g c p) f -> g p c f", c=G, p=P)
        o_v = attn.rearrange("(g c p) f -> g p c f", c=G, p=P)
        xo_v = x_dram.rearrange("(g c p) f -> g p c f", c=G, p=P)
        y_v = y_dram.rearrange("(c p) f -> c p f", p=P)

        @block.sync
        def _(sp):
            for k, w in enumerate((w_self, w_neigh)):
                sp.dma_start(w_rows[:, k, :, :], w.rearrange("(c p) f -> p c f", p=P)).then_inc(w_loaded, 16)
            with sp.Fori(0, NG // 2) as r:
                for b in range(2):
                    sp.wait_ge(turned[b], ONE + G * r)
                    sp.wait_ge(x_stored[b], ONE + 16 * r)
                    sp.dma_start(x[:, b, :, :], x_v[2 * r + b]).then_inc(x_loaded[b], 16)
                    sp.dma_start(o[:, b, :, :], o_v[2 * r + b]).then_inc(x_loaded[b], 16)

        @block.vector
        def _(dve):
            dve.wait_ge(w_loaded, ONE + 32)
            nc.vector.tensor_reduce(rn[:, :], w_rows[:, 1, :, :], AX.X, ALU.add).then_inc(rn_ready, 1)
            dve.wait_ge(rn_ready, ONE + 1)
            nc.vector.tensor_copy(rn_b[:, :, :], rn[:, :].rearrange("p (c o) -> p c o", o=1).to_broadcast([P, KC, P]))\
                .then_inc(rnb_ready, 1)
            with dve.Fori(0, NG // 2) as r:
                for b in range(2):
                    g = 2 * r + b
                    dve.wait_ge(x_loaded[b], ONE + 32 * r + 32)
                    add_elu(nc, dve, g, x[:, b, :, :], o[:, b, :, :], neg, eluw)
                    dve.wait_ge(eluw["added"], ONE + 2 * g + 2)
                    norm.rows(dve, g, x, b)
                    dve.wait_ge(norm.ready, ONE + G * g + G)
                    nc.vector.tensor_copy(x0[:, bass.ds(G * g, G)], x[:, b, :, 0]).then_inc(x0_ready, 1)

        @block.scalar
        def _(act):
            def exps(g):
                act.wait_ge(eluw["neg"], ONE + g + 1)
                nc.scalar.activation(neg[:, :, :], neg[:, :, :], ACT.Exp).then_inc(eluw["exp"], 1)
                norm.rsqrt(act, g)

            def products(g, r, b):
                act.wait_ge(x0_ready, ONE + g + 1)
                act.dma_start(xo_v[g], x[:, b, :, :]).then_inc(x_stored[b], 16)
                for c in range(G):
                    act.wait_ge(turned[b], ONE + G * r + c + 1)
                    act.wait_ge(y_done, ONE + G * g + c - 1 if c else ONE + G * g)
                    nc.scalar.activation(xT[:, c % 2, :, :], pT[c % 2][:, :, :], ACT.Copy).then_inc(xT_ready, 1)
                    act.wait_ge(y_done, ONE + G * g + c + 1)
                    act.wait_ge(y_stored[c % 2], ONE + 16 * (2 * g + c // 2))
                    nc.scalar.activation(ys[:, c % 2, :], pW[c % 2][:, :], ACT.Copy).then_inc(y_copied, 1)
                    act.wait_ge(y_copied, ONE + G * g + c + 1)
                    act.dma_start(y_v[G * g + c], ys[:, c % 2, :]).then_inc(y_stored[c % 2], 16)

            for c in range(KC):
                act.wait_ge(w_turned, ONE + c + 1)
                nc.scalar.activation(wT[:, c, :], pT[c % 2][:, :, :].rearrange("p c f -> p (c f)"), ACT.Copy).then_inc(wT_ready, 1)
            act.wait_ge(r_done, ONE + 1)
            nc.scalar.activation(r_bc[:, :], pW[0][:, :], ACT.Copy).then_inc(r_copied, 1)
            exps(0)
            with act.Fori(0, NG // 2 - 1) as r:
                exps(2 * r + 1)
                products(2 * r, r, 0)
                exps(2 * r + 2)
                products(2 * r + 1, r, 1)
            exps(NG - 1)
            products(NG - 2, NG // 2 - 1, 0)
            products(NG - 1, NG // 2 - 1, 1)
            for b in range(2):
                act.wait_ge(y_stored[b], ONE + 16 * (NC // 2))
                act.wait_ge(x_stored[b], ONE + 16 * (NG // 2))

        @block.tensor
        def _(pe):
            pe.wait_ge(w_loaded, ONE + 32)
            for c in range(KC):
                if c >= 2:
                    pe.wait_ge(wT_ready, ONE + c - 1)
                for k in range(KC):
                    last = nc.tensor.transpose(pT[c % 2][:, k, :], w_rows[:, 0, k, c * P:(c + 1) * P], ident[:, :])
                last.then_inc(w_turned, 1)
            pe.wait_ge(rnb_ready, ONE + 1)
            for c in range(KC):
                last = nc.tensor.matmul(pW[0][:, c * P:(c + 1) * P], rn_b[:, c, :], ident[:, :], start=True, stop=True)
            last.then_inc(r_done, 1)
            pe.wait_ge(r_copied, ONE + 1)
            pe.wait_ge(wT_ready, ONE + KC)
            with pe.Fori(0, NG // 2) as r:
                for b in range(2):
                    g = 2 * r + b
                    for c in range(G):
                        pe.wait_ge(norm.ready, ONE + G * g + c + 1)
                        if c < 2:
                            pe.wait_ge(xT_ready, ONE + G * g)
                        else:
                            pe.wait_ge(xT_ready, ONE + G * g + c - 1)
                        for kc in range(KC):
                            last = nc.tensor.transpose(pT[c % 2][:, kc, :], x[:, b, c, kc * P:(kc + 1) * P], ident[:, :])
                        last.then_inc(turned[b], 1)
                        pe.wait_ge(xT_ready, ONE + G * g + c + 1)
                        if c < 2:
                            pe.wait_ge(y_copied, ONE + G * g)
                        else:
                            pe.wait_ge(y_copied, ONE + G * g + c - 1)
                        for kc in range(KC):
                            last = nc.tensor.matmul(pW[c % 2][:, :], xT[:, c % 2, kc, :], wT[:, kc, :],
                                                    start=kc == 0, stop=kc == KC - 1)
                        last.then_inc(y_done, 1)
    free_semaphores(nc, sems)


def neighbour_sums(nc, code, ident_bf, x0, s_col):
    ctx = ExitStack()
    with ctx:
        def sb(name, shape, dt):
            return ctx.enter_context(nc.sbuf_tensor(f"{name}_3b", shape, dt))

        sems = []

        def sem(name):
            sems.append(nc.alloc_semaphore(f"{name}_3b"))
            return sems[-1]

        CUT = 2432
        parts = sb("parts", [P, NC, 3], BF16)
        rest = sb("rest", [P, 2, NC], F32)
        ones = [sb(f"ones{b}", [P, N], BF16) for b in range(2)]
        acc = ctx.enter_context(nc.psum_tensor("acc_3b", [P, NC, 16], F32))
        split, dve_ones, act_ones = sem("split"), sem("dve_ones"), sem("act_ones")
        used = [sem(f"used{b}") for b in range(2)]
        summed = sem("summed")
        start_at_one(nc, sems)
        block = ctx.enter_context(nc.Block())

        @block.vector
        def _(dve):
            nc.vector.tensor_copy(parts[:, :, 0], x0[:, :]).then_inc(split, 1)
            dve.wait_ge(split, ONE + 1)
            nc.vector.tensor_tensor(rest[:, 0, :], x0[:, :], parts[:, :, 0], ALU.subtract).then_inc(split, 1)
            dve.wait_ge(split, ONE + 2)
            nc.vector.tensor_copy(parts[:, :, 1], rest[:, 0, :]).then_inc(split, 1)
            dve.wait_ge(split, ONE + 3)
            nc.vector.tensor_tensor(rest[:, 1, :], rest[:, 0, :], parts[:, :, 1], ALU.subtract).then_inc(split, 1)
            dve.wait_ge(split, ONE + 4)
            nc.vector.tensor_copy(parts[:, :, 2], rest[:, 1, :]).then_inc(split, 1)
            with dve.Fori(0, NC // 2) as t:
                for b in range(2):
                    dve.wait_ge(used[b], ONE + t)
                    nc.vector.tensor_scalar(ones[b][:, 0:CUT], code[:, 2 * t + b, 0:CUT], 0.0, None, ALU.max).then_inc(dve_ones, 1)
            for b in range(2):
                dve.wait_ge(used[b], ONE + NC // 2)
            nc.vector.tensor_reduce(s_col[:, :], acc[:, :, 0:3], AX.X, ALU.add).then_inc(summed, 1)

        @block.scalar
        def _(act):
            with act.Fori(0, NC // 2) as t:
                for b in range(2):
                    act.wait_ge(used[b], ONE + t)
                    nc.scalar.activation(ones[b][:, CUT:N], code[:, 2 * t + b, CUT:N], ACT.Relu).then_inc(act_ones, 1)

        @block.tensor
        def _(pe):
            nc.tensor.matmul(acc[:, NC - 1, 14:16], ident_bf[:, :], ident_bf[:, 0:2], start=True, stop=True, skip_group_check=True)
            pe.wait_ge(split, ONE + 5)
            with pe.Fori(0, NC // 2) as t:
                for b in range(2):
                    pe.wait_ge(dve_ones, ONE + 2 * t + b + 1)
                    pe.wait_ge(act_ones, ONE + 2 * t + b + 1)
                    for c in range(NC):
                        last = nc.tensor.matmul(acc[:, c, 0:3], ones[b][:, c * P:(c + 1) * P], parts[:, 2 * t + b, :],
                                                start=False, stop=False, skip_group_check=True)
                    last.then_inc(used[b], 1)
    free_semaphores(nc, sems)


def combine(nc, G, NG, y_dram, x_dram, r_bc, s_col, out):
    ctx = ExitStack()
    with ctx:
        def sb(name, shape, dt):
            return ctx.enter_context(nc.sbuf_tensor(f"{name}_3c", shape, dt))

        sems = []

        def sem(name):
            sems.append(nc.alloc_semaphore(f"{name}_3c"))
            return sems[-1]

        x = sb("x", [P, 2, G, F], F32)
        y = sb("y", [P, 2, G, F], F32)
        norm = Norm(nc, sb, sem, G)
        loaded = [sem(f"loaded{b}") for b in range(2)]
        stored = [sem(f"stored{b}") for b in range(2)]
        y_step, added = sem("y_step"), sem("added")
        start_at_one(nc, sems)
        block = ctx.enter_context(nc.Block())
        x_v = x_dram.rearrange("(g c p) f -> g p c f", c=G, p=P)
        y_v = y_dram.rearrange("(g c p) f -> g p c f", c=G, p=P)
        out_v = out.rearrange("(g c p) f -> g p c f", c=G, p=P)

        @block.sync
        def _(sp):
            with sp.Fori(0, NG // 2) as r:
                for b in range(2):
                    sp.wait_ge(stored[b], ONE + 16 * r)
                    sp.dma_start(x[:, b, :, :], x_v[2 * r + b]).then_inc(loaded[b], 16)
                    sp.dma_start(y[:, b, :, :], y_v[2 * r + b]).then_inc(loaded[b], 16)

        @block.scalar
        def _(act):
            with act.Fori(0, NG // 2) as r:
                for b in range(2):
                    g = 2 * r + b
                    norm.rsqrt(act, g)
                    act.wait_ge(norm.ready, ONE + G * g + G)
                    act.dma_start(out_v[g], x[:, b, :, :]).then_inc(stored[b], 16)
            for b in range(2):
                act.wait_ge(stored[b], ONE + 16 * (NG // 2))

        @block.vector
        def _(dve):
            with dve.Fori(0, NG // 2) as r:
                for b in range(2):
                    g = 2 * r + b
                    dve.wait_ge(loaded[b], ONE + 32 * r + 32)
                    for c in range(G):
                        nc.vector.scalar_tensor_tensor(y[:, b, c, :], r_bc[:, :], s_col[:, bass.ds(G * g + c, 1)],
                                                       y[:, b, c, :], ALU.mult, ALU.add).then_inc(y_step, 1)
                    dve.wait_ge(y_step, ONE + G * g + G)
                    nc.vector.scalar_tensor_tensor(x[:, b, :, :], y[:, b, :, :], 0.0, x[:, b, :, :], ALU.max, ALU.add)\
                        .then_inc(added, 1)
                    dve.wait_ge(added, ONE + g + 1)
                    norm.rows(dve, g, x, b)
    free_semaphores(nc, sems)


def gat_kernel(nc, x, adj, W0, a1, a2, W1, a, W2, a_l, a_r, w_self, w_neigh, out):
    def dram(name, shape, dt):
        return nc.dram_tensor(name, shape, dt, kind="Internal").ap()

    f1_dram = dram("f1_rows", (8, N), F32)
    v_dram = dram("values", (N, 8 * 4 * 65), F16)
    attn = dram("attended", (N, F), F32)
    y_dram = dram("self_products", (N, F), F32)
    rows = [dram(f"rows{k}", (N, F), F32) for k in range(2)]

    ctx = ExitStack()
    with ctx:
        def sb(name, shape, dt):
            return ctx.enter_context(nc.sbuf_tensor(name, shape, dt))

        code = sb("code", [P, NC, N], I8)
        f12 = sb("f12", [P, NC, 16], F32)
        beta = sb("beta", [P, NC, 2, 8], BF16)
        rowf = sb("rowf", [P, NC, 16], F32)
        ident = sb("ident", [P, P], F32)
        ident_bf = sb("ident_bf", [P, P], BF16)
        cols = (f12, beta, rowf)
        made = ctx.enter_context(nc.semaphore("ident_made"))
        with nc.Block() as block:
            @block.gpsimd
            def _(pool):
                nc.gpsimd.memset(ident[:, :], 0.0).then_inc(made, 1)
                nc.gpsimd.memset(ident_bf[:, :], 0.0).then_inc(made, 1)
                pool.wait_ge(made, 2)
                for m in (ident, ident_bf):
                    nc.gpsimd.affine_select(out=m[:, :], in_=m[:, :], compare_op=ALU.not_equal, fill=1.0, base=0,
                                            pattern=[[-1, P]], channel_multiplier=1).then_inc(made, 1)
                pool.wait_ge(made, 4)

        eight, four = Layer(8), Layer(4)
        load_adjacency(nc, adj, code, ident_bf)
        w0 = [W0[:, k * P:(k + 1) * P, :].rearrange("h k o -> k h o") for k in range(KC)]
        w1 = [W1[k * P:(k + 1) * P, :] for k in range(KC)]
        w2 = [W2[k * P:(k + 1) * P, :] for k in range(KC)]
        flat = [a1.rearrange("h o -> (h o)"), a2.rearrange("h o -> (h o)")]
        prepare(nc, eight, 0, x, None, False, w0, *flat, None, v_dram, f1_dram, cols, ident)
        attend(nc, eight, 0, code, v_dram, f1_dram, attn, cols, ident_bf)
        flat = [a[0, :, k * 64:(k + 1) * 64] for k in range(2)]
        prepare(nc, eight, 1, x, attn, False, w1, *flat, rows[0], v_dram, f1_dram, cols, ident)
        attend(nc, eight, 1, code, v_dram, f1_dram, attn, cols, ident_bf)
        flat = [m.rearrange("h o -> (h o)") for m in (a_l, a_r)]
        prepare(nc, four, 2, rows[0], attn, True, w2, *flat, rows[1], v_dram, f1_dram, cols, ident)
        attend(nc, four, 2, code, v_dram, f1_dram, attn, cols, ident_bf)
        last_layer(nc, rows[1], attn, w_self, w_neigh, code, y_dram, rows[0], out, ident, ident_bf)


_INS = ['x', 'adj', 'L0_gnn_W', 'L0_gnn_a1', 'L0_gnn_a2', 'L1_gnn_W', 'L1_gnn_a', 'L2_gnn_W', 'L2_gnn_a_l', 'L2_gnn_a_r',
        'L3_gnn_w_self', 'L3_gnn_w_neigh']


def kernel(**inputs):
    import numpy as np
    import concourse.bacc as bacc
    from concourse.bass_utils import run_bass_kernel_spmd

    nc = bacc.Bacc("TRN2", target_bir_lowering=False, num_devices=1,
                   dynamic_dma_scratch_size=4096)
    arrays, args = {}, []
    for name in _INS:
        a = np.ascontiguousarray(inputs[name])
        arrays[f"in_{name}"] = a
        args.append(nc.dram_tensor(f"in_{name}", a.shape, mybir.dt.from_np(a.dtype), kind="ExternalInput").ap())
    args.append(nc.dram_tensor("out_0", (N, F), F32, kind="ExternalOutput").ap())
    gat_kernel(nc, *args)
    r = run_bass_kernel_spmd(nc, [arrays], core_ids=[0])
    return r.results[0]["out_0"]
```

```python
import concourse.bass as bass
from concourse import mybir
from contextlib import ExitStack

F32 = mybir.dt.float32
BF16 = mybir.dt.bfloat16
F16 = mybir.dt.float16
I32 = mybir.dt.int32
ALU = mybir.AluOpType
ACT = mybir.ActivationFunctionType
AX = mybir.AxisListType

N = 4096
F = 512
P = 128
NC = N // P
KC = F // P
EPS = 1e-5
SLOPE = 0.2
VSCALE = 512.0
ONE = 1
TINY = 1e-30


def start_at_one(nc, sems):
    for s in sems:
        nc.gpsimd.sem_inc(s, ONE)
    nc.all_engine_barrier()


def free_semaphores(nc, sems):
    nc.clear_and_free_semaphores(sems)
    nc.all_engine_barrier()


class Layer:

    def __init__(self, heads):
        self.H = heads
        self.D = F // heads
        self.VW = 2 * 2 * (self.D + 1)
        self.CPB = 512 // (2 * (self.D + 1))
        if self.CPB == 3:
            self.CPB = 2
        self.IB = 8 * self.CPB * P
        self.NIB = N // self.IB
        self.CB = self.IB // P


def load_adjacency(nc, adj, mask, mask_dram, ident_bf):
    ctx = ExitStack()
    with ctx:
        raw = [ctx.enter_context(nc.sbuf_tensor(f"adj_raw{b}", [P, N], I32)) for b in range(2)]
        one = [ctx.enter_context(nc.sbuf_tensor(f"adj_one{b}", [P, N], BF16)) for b in range(2)]
        G = 4
        odd = [ctx.enter_context(nc.sbuf_tensor(f"adj_odd{b}", [P, NC // 2, G * P], BF16)) for b in range(2)]
        turned = [[ctx.enter_context(nc.psum_tensor(f"adj_turned{b}{g}", [P, 8, P], BF16)) for g in range(4)]
                  for b in range(2)]
        sems = []

        def sem(name):
            sems.append(nc.alloc_semaphore(name))
            return sems[-1]

        loaded = [sem(f"adj_loaded{b}") for b in range(2)]
        converted = [sem(f"adj_converted{b}") for b in range(2)]
        bank_turned = [sem(f"adj_bank_turned{b}") for b in range(2)]
        kept = [sem(f"adj_kept{b}") for b in range(2)]
        staged = [sem(f"adj_staged{b}") for b in range(2)]
        stored = [sem(f"adj_stored{s}") for s in range(2)]
        start_at_one(nc, sems)
        block = ctx.enter_context(nc.Block())
        dram_v = mask_dram.rearrange("c p (g i) -> g p c i", i=G * P)

        @block.sync
        def _(sp):
            with sp.Fori(0, NC // 2) as t:
                for b in range(2):
                    sp.wait_ge(converted[b], ONE + t)
                    sp.dma_start(raw[b][:, :], adj[bass.ds((2 * t + b) * P, P), :]).then_inc(loaded[b], 16)

        @block.vector
        def _(dve):
            with dve.Fori(0, NC // 2) as t:
                for b in range(2):
                    dve.wait_ge(loaded[b], ONE + 16 * t + 16)
                    dve.wait_ge(bank_turned[b], ONE + 4 * t)
                    nc.vector.tensor_scalar(one[b][:, :], raw[b][:, :], 0.0, None, ALU.is_gt)\
                        .then_inc(converted[b], 1)
                    for g in range(2):
                        dve.wait_ge(bank_turned[b], ONE + 4 * t + g + 1)
                        nc.vector.tensor_copy(mask[:, 8 * g:8 * g + 8, bass.ds((2 * t + b) * P, P)],
                                              turned[b][g][:, :, :]).then_inc(kept[b], 1)

        @block.scalar
        def _(act):
            with act.Fori(0, NC // (2 * G)) as t:
                for s in range(2):
                    act.wait_ge(stored[s], ONE + 16 * t)
                    for c in range(G):
                        b = c % 2
                        for g in range(2, 4):
                            act.wait_ge(bank_turned[b], ONE + 4 * (4 * t + 2 * s + c // 2) + g + 1)
                            nc.scalar.activation(odd[s][:, 8 * (g - 2):8 * (g - 2) + 8, c * P:(c + 1) * P],
                                                 turned[b][g][:, :, :], ACT.Copy).then_inc(staged[b], 1)
                    for b in range(2):
                        act.wait_ge(staged[b], ONE + 2 * (4 * t + 2 * s + 2))
                    act.dma_start(dram_v[2 * t + s], odd[s][:, :, :]).then_inc(stored[s], 16)
            for s in range(2):
                act.wait_ge(stored[s], ONE + 16 * (NC // (2 * G)))

        @block.tensor
        def _(pe):
            with pe.Fori(0, NC // 2) as t:
                for b in range(2):
                    pe.wait_ge(converted[b], ONE + t + 1)
                    pe.wait_ge(kept[b], ONE + 2 * t)
                    pe.wait_ge(staged[b], ONE + 2 * t)
                    for g in range(4):
                        for c in range(8):
                            j = (2 * (8 * (g % 2) + c) + g // 2) * P
                            last = nc.tensor.transpose(turned[b][g][:, c, :], one[b][:, j:j + P], ident_bf[:, :])
                        last.then_inc(bank_turned[b], 1)

    free_semaphores(nc, sems)


class Norm:

    def __init__(self, nc, sb, sem, G):
        self.nc, self.G = nc, G
        self.stats = sb("stats", [P, G, 6], F32)
        self.mt = sb("mt", [P, 5, G], F32)
        self.mean = sb("mean", [P, G], F32)
        self.ve = sb("ve", [P, G], F32)
        self.lnv = sb("lnv", [P, G], F32)
        self.rs0 = sb("rs0", [P, G], F32)
        self.rt = sb("rt", [P, 3, G], F32)
        self.rs = sb("rs", [P, G], F32)
        self.step = sem("norm_step")
        self.STEPS = G + 10
        self.ve_ready, self.ln_done, self.rs0_ready = sem("ve_ready"), sem("ln_done"), sem("rs0_ready")
        self.ready = sem("x_ready")

    def rows(self, dve, g, x, b):
        nc, G, step, base = self.nc, self.G, self.step, ONE + self.STEPS * g
        st, mt = self.stats, self.mt
        for c in range(G):
            nc.vector.bn_stats(st[:, c, :], x[:, b, c, :]).then_inc(step, 1)
        dve.wait_ge(self.ready, ONE + G * g)
        dve.wait_ge(step, base + G)
        nc.vector.tensor_tensor(mt[:, 0, :], st[:, :, 1], st[:, :, 4], ALU.subtract).then_inc(step, 1)
        nc.vector.tensor_tensor(mt[:, 1, :], st[:, :, 1], st[:, :, 4], ALU.add).then_inc(step, 1)
        nc.vector.tensor_tensor(mt[:, 2, :], st[:, :, 2], st[:, :, 5], ALU.add).then_inc(step, 1)
        dve.wait_ge(step, base + G + 3)
        nc.vector.tensor_tensor(mt[:, 3, :], mt[:, 0, :], mt[:, 0, :], ALU.mult).then_inc(step, 1)
        nc.vector.tensor_scalar(mt[:, 4, :], mt[:, 2, :], 1.0 / F, EPS, ALU.mult, ALU.add).then_inc(step, 1)
        nc.vector.tensor_scalar(self.mean[:, :], mt[:, 1, :], 0.5, None, ALU.mult).then_inc(step, 1)
        dve.wait_ge(step, base + G + 6)
        nc.vector.scalar_tensor_tensor(self.ve[:, :], mt[:, 3, :], 0.25, mt[:, 4, :], ALU.mult, ALU.add).then_inc(self.ve_ready, 1)
        dve.wait_ge(self.rs0_ready, ONE + g + 1)
        nc.vector.tensor_tensor(self.rt[:, 0, :], self.rs0[:, :], self.rs0[:, :], ALU.mult).then_inc(step, 1)
        dve.wait_ge(step, base + G + 6 + 1)
        nc.vector.tensor_tensor(self.rt[:, 1, :], self.rt[:, 0, :], self.ve[:, :], ALU.mult).then_inc(step, 1)
        dve.wait_ge(step, base + G + 6 + 2)
        nc.vector.tensor_scalar(self.rt[:, 2, :], self.rt[:, 1, :], -0.5, 1.5, ALU.mult, ALU.add).then_inc(step, 1)
        dve.wait_ge(step, base + G + 6 + 3)
        nc.vector.tensor_tensor(self.rs[:, :], self.rt[:, 2, :], self.rs0[:, :], ALU.mult).then_inc(step, 1)
        dve.wait_ge(step, base + G + 6 + 4)
        for c in range(G):
            nc.vector.tensor_scalar(x[:, b, c, :], x[:, b, c, :], self.mean[:, c:c + 1], self.rs[:, c:c + 1],
                                    ALU.subtract, ALU.mult).then_inc(self.ready, 1)

    def rsqrt(self, act, g):
        act.wait_ge(self.ve_ready, ONE + g + 1)
        self.nc.scalar.activation(self.lnv[:, :], self.ve[:, :], ACT.Ln).then_inc(self.ln_done, 1)
        act.wait_ge(self.ln_done, ONE + g + 1)
        self.nc.scalar.activation(self.rs0[:, :], self.lnv[:, :], ACT.Exp, scale=-0.5).then_inc(self.rs0_ready, 1)


def add_elu(nc, dve, g, xg, og, neg, sems):
    dve.wait_ge(sems["added"], ONE + 2 * g)
    nc.vector.tensor_scalar(neg[:, :, :], og, 0.0, None, ALU.min).then_inc(sems["neg"], 1)
    nc.vector.scalar_tensor_tensor(xg, og, 0.0, xg, ALU.max, ALU.add).then_inc(sems["added"], 1)
    dve.wait_ge(sems["exp"], ONE + g + 1)
    dve.wait_ge(sems["added"], ONE + 2 * g + 1)
    nc.vector.scalar_tensor_tensor(xg, neg[:, :, :], -1.0, xg, ALU.add, ALU.add).then_inc(sems["added"], 1)


def prepare(nc, lay, number, x_in, attn, elu, w, a_src, a_dst, x_out, v_dram, f1_dram, cols, ident):
    H, D = lay.H, lay.D
    f12, beta, ndelta, rowf = cols
    G = 4
    NG = NC // G
    ln = attn is not None
    LOADS = 16 * (2 if ln else 1)
    ctx = ExitStack()
    with ctx:
        def sb(name, shape, dt):
            return ctx.enter_context(nc.sbuf_tensor(f"{name}_{number}", shape, dt))

        def ps(name, shape, dt):
            return ctx.enter_context(nc.psum_tensor(f"{name}_{number}", shape, dt))

        sems = []

        def sem(name):
            sems.append(nc.alloc_semaphore(f"{name}_{number}"))
            return sems[-1]

        w_sb = sb("w_sb", [P, KC, F], F32)
        wa_tmp = sb("wa_tmp", [P, KC, F], F32)
        a_bc = sb("a_bc", [P, 2, F], F32)
        wa = sb("wa", [P, KC, 2 * H], F32)
        x = sb("x", [P, 2, G, F], F32)
        if ln:
            o = sb("o", [P, 2, G, F], F32)
            neg = wa_tmp
            norm = Norm(nc, sb, sem, G)
            eluw = {k: sem(f"elu_{k}") for k in ("neg", "exp", "added")}
            x_ready = norm.ready
        xT = sb("xT", [P, G, KC, P], F32)
        fst = sb("fst", [P, G, 2 * H], F32)
        fT = sb("fT", [2 * H, G, P], I32)
        ebd = sb("ebd", [P, G, 2, H], F32)
        ebr = sb("ebr", [P, G, 2, H], BF16)
        rec = sb("rec", [P, G, 2, H], F32)
        rho = sb("rho", [P, G, 2, H], F32)
        vf = [sb(f"vf{b}", [P, H, 2, D + 1], F32) for b in range(2)]
        vh = [sb(f"vh{b}", [P, H, 2, 2, D + 1], F16) for b in range(2)]
        rfm = sb("rfm", [P, NC, H, 2], F32)
        pT = [ps(f"pT{b}", [P, KC, P], F32) for b in range(2)]
        pW = [ps(f"pW{c}", [P, F], F32) for c in range(G)]
        pF = ps("pF", [P, G, P], F32)[:, :, 0:2 * H]
        pFT_f = ps("pFT", [P, G, P], F32)[0:2 * H, :, :]
        pFT = pFT_f.bitcast(I32)

        w_loaded, a_loaded = sem("w_loaded"), sem("a_loaded")
        wa_step, wa_ready = sem("wa_step"), sem("wa_ready")
        x_loaded = [sem(f"x_loaded{b}") for b in range(2)]
        x_stored = [sem(f"x_stored{b}") for b in range(2)]
        turned = [sem(f"turned{b}") for b in range(2)]
        xT_ready = sem("xT_ready")
        f_done, f_copied = sem("f_done"), sem("f_copied")
        fT_done, fT_copied, fT_stored = sem("fT_done"), sem("fT_copied"), sem("fT_stored")
        wx_done, rho_step, v_ready = sem("wx_done"), sem("rho_step"), sem("v_ready")
        high_ready, low_ready = sem("high_ready"), sem("low_ready")
        v_stored = [sem(f"v_stored{b}") for b in range(2)]
        rf_step, rf_ready = sem("rf_step"), sem("rf_ready")
        start_at_one(nc, sems)
        block = ctx.enter_context(nc.Block())

        x_v = x_in.rearrange("(g c p) f -> g p c f", c=G, p=P)
        o_v = attn.rearrange("(g c p) f -> g p c f", c=G, p=P) if ln else None
        xo_v = x_out.rearrange("(g c p) f -> g p c f", c=G, p=P) if ln else None
        f1_v = f1_dram[0:H, :].rearrange("h (g c p) -> g h c p", c=G, p=P)
        v_v = v_dram[:, 0:H * lay.VW].rearrange("(c p) m -> c p m", p=P)

        @block.sync
        def _(sp):
            for kc in range(KC):
                dst = w_sb[:, kc, :]
                sp.dma_start(dst if len(w[kc].shape) == 2 else dst.rearrange("p (h o) -> p h o", h=H), w[kc])\
                    .then_inc(w_loaded, 16)
            for k, a in enumerate((a_src, a_dst)):
                dst = a_bc[:, k, :] if len(a.shape) == 1 else a_bc[:, k, :].rearrange("p (h o) -> p h o", h=H)
                sp.dma_start(dst, a.partition_broadcast(P)).then_inc(a_loaded, 16)
            with sp.Fori(0, NG // 2) as r:
                for b in range(2):
                    sp.wait_ge(turned[b], ONE + G * r)
                    if ln:
                        sp.wait_ge(x_stored[b], ONE + 16 * r)
                    sp.dma_start(x[:, b, :, :], x_v[2 * r + b]).then_inc(x_loaded[b], 16)
                    if ln:
                        sp.dma_start(o[:, b, :, :], o_v[2 * r + b]).then_inc(x_loaded[b], 16)

        @block.vector
        def _(dve):
            dve.wait_ge(w_loaded, ONE + 16 * KC)
            dve.wait_ge(a_loaded, ONE + 32)
            for k in range(2):
                nc.vector.tensor_tensor(wa_tmp[:, :, :], w_sb[:, :, :],
                                        a_bc[:, k:k + 1, :].to_broadcast([P, KC, F]), ALU.mult).then_inc(wa_step, 1)
                dve.wait_ge(wa_step, ONE + 2 * k + 1)
                nc.vector.tensor_reduce(wa[:, :, k * H:(k + 1) * H],
                                        wa_tmp[:, :, :].rearrange("p k (h o) -> p k h o", h=H), AX.X, ALU.add)\
                    .then_inc(wa_step, 1)
                dve.wait_ge(wa_step, ONE + 2 * k + 2)

            def layernorm(g, r, b):
                dve.wait_ge(x_loaded[b], ONE + LOADS * r + LOADS)
                xg, og = x[:, b, :, :], o[:, b, :, :]
                if elu:
                    add_elu(nc, dve, g, xg, og, neg, eluw)
                else:
                    nc.vector.tensor_tensor(xg, og, xg, ALU.add).then_inc(eluw["added"], 2)
                dve.wait_ge(eluw["added"], ONE + 2 * g + 2)
                norm.rows(dve, g, x, b)

            def values(g):
                dve.wait_ge(f_copied, ONE + 4 * g + 4)
                nc.vector.tensor_copy(ebr[:, :, :, :], ebd[:, :, :, :]).then_inc(rho_step, 1)
                dve.wait_ge(rho_step, ONE + 4 * g + 1)
                nc.vector.reciprocal(rec[:, :, :, :], ebr[:, :, :, :]).then_inc(rho_step, 1)
                nc.vector.tensor_copy(beta[:, bass.ds(G * g, G), :, 0:H], ebr[:, :, :, :]).then_inc(rho_step, 1)
                dve.wait_ge(rho_step, ONE + 4 * g + 3)
                nc.vector.scalar_tensor_tensor(rho[:, :, :, :], ebd[:, :, :, :], VSCALE, rec[:, :, :, :],
                                               ALU.mult, ALU.mult).then_inc(rho_step, 1)
                dve.wait_ge(rho_step, ONE + 4 * g + 4)
                for c in range(G):
                    b = c % 2
                    if c >= 2:
                        dve.wait_ge(high_ready, ONE + G * g + c - 1)
                        dve.wait_ge(low_ready, ONE + G * g + c - 1)
                    else:
                        dve.wait_ge(low_ready, ONE + G * g)
                        dve.wait_ge(high_ready, ONE + G * g)
                    nc.vector.tensor_copy(vf[b][:, :, :, D:D + 1],
                                          rho[:, c, :, :].rearrange("p k (h o) -> p h k o", o=1)).then_inc(v_ready, 1)
                    dve.wait_ge(wx_done, ONE + G * g + c + 1)
                    for k in range(2):
                        nc.vector.tensor_tensor(vf[b][:, :, k, 0:D], pW[c][:, :].rearrange("p (h o) -> p h o", h=H),
                                                rho[:, c, k, :].rearrange("p (h o) -> p h o", o=1).to_broadcast([P, H, D]), ALU.mult)\
                            .then_inc(v_ready, 1)

                dve.wait_ge(fT_done, ONE + g + 1)
                dve.wait_ge(fT_stored, ONE + 16 * g)
                nc.vector.tensor_scalar(fT[:, :, :], pFT, -2, None, ALU.bitwise_and).then_inc(fT_copied, 1)

            if ln:
                layernorm(0, 0, 0)
                with dve.Fori(0, NG // 2 - 1) as r:
                    layernorm(2 * r + 1, r, 1)
                    values(2 * r)
                    layernorm(2 * r + 2, r + 1, 0)
                    values(2 * r + 1)
                layernorm(NG - 1, NG // 2 - 1, 1)
                values(NG - 2)
                values(NG - 1)
            else:
                with dve.Fori(0, NG) as g:
                    values(g)
            f1 = f12[:, :, 0:H]
            for k, s in enumerate((1.0 - SLOPE, SLOPE - 1.0)):
                nc.vector.tensor_scalar(rfm[:, :, :, k], f1, s, 0.0, ALU.mult, ALU.min).then_inc(rf_step, 1)
            f2 = f12[:, :, H:2 * H]
            nc.vector.tensor_scalar(f2, f2, TINY, None, ALU.add).then_inc(rf_step, 1)
            nc.vector.tensor_scalar(ndelta[:, :, 0:H], beta[:, :, 1, 0:H], -1.0, None, ALU.mult).then_inc(rf_step, 1)
            dve.wait_ge(rf_step, ONE + 4)
            nc.vector.tensor_scalar(f2.bitcast(I32), f2.bitcast(I32), 1, None, ALU.bitwise_or).then_inc(rf_step, 1)

        @block.scalar
        def _(act):
            def rsqrt(g):
                if elu:
                    act.wait_ge(eluw["neg"], ONE + g + 1)
                    nc.scalar.activation(neg[:, :, :], neg[:, :, :], ACT.Exp).then_inc(eluw["exp"], 1)
                norm.rsqrt(act, g)

            def turn(g, r, b):
                act.wait_ge(wx_done, ONE + G * g)
                for c in range(G):
                    act.wait_ge(turned[b], ONE + G * r + c + 1)
                    nc.scalar.activation(xT[:, c, :, :], pT[c % 2][:, :, :], ACT.Copy).then_inc(xT_ready, 1)
                act.wait_ge(f_done, ONE + g + 1)
                act.wait_ge(fT_done, ONE + g)
                nc.scalar.activation(fst[:, :, :], pF, ACT.Copy).then_inc(f_copied, 1)
                nc.scalar.activation(f12[:, bass.ds(G * g, G), 0:2 * H], pF, ACT.Copy).then_inc(f_copied, 1)
                act.wait_ge(rho_step, ONE + 4 * g)
                nc.scalar.activation(ebd[:, :, 0, :], pF[:, :, H:2 * H], ACT.Exp).then_inc(f_copied, 1)
                nc.scalar.activation(ebd[:, :, 1, :], pF[:, :, H:2 * H], ACT.Exp, scale=SLOPE).then_inc(f_copied, 1)

            def high(g):
                def store(c):
                    act.wait_ge(low_ready, ONE + G * g + c + 1)
                    act.dma_start(v_v[G * g + c], vh[c % 2][:, :, :, :, :].rearrange("p h k s d -> p (h k s d)"))\
                        .then_inc(v_stored[c % 2], 16)

                for c in range(G):
                    b = c % 2
                    act.wait_ge(v_stored[b], ONE + 16 * (2 * g + c // 2))
                    act.wait_ge(v_ready, ONE + 3 * (G * g + c) + 3)
                    nc.scalar.activation(vh[b][:, :, :, 0, :], vf[b][:, :, :, :], ACT.Copy).then_inc(high_ready, 1)
                    if c:
                        store(c - 1)
                store(G - 1)
                act.wait_ge(fT_copied, ONE + g + 1)
                act.dma_start(f1_v[g], fT[0:H, :, :].bitcast(F32)).then_inc(fT_stored, 16)

            def store_rows(g, r, b):
                act.wait_ge(x_ready, ONE + G * (g + 1))
                act.dma_start(xo_v[g], x[:, b, :, :]).then_inc(x_stored[b], 16)

            def rows(g, r, b):
                if ln:
                    rsqrt(g)
                    store_rows(g, r, b)

            rows(0, 0, 0)
            turn(0, 0, 0)
            with act.Fori(0, NG // 2 - 1) as r:
                rows(2 * r + 1, r, 1)
                high(2 * r)
                turn(2 * r + 1, r, 1)
                rows(2 * r + 2, r + 1, 0)
                high(2 * r + 1)
                turn(2 * r + 2, r + 1, 0)
            rows(NG - 1, NG // 2 - 1, 1)
            high(NG - 2)
            turn(NG - 1, NG // 2 - 1, 1)
            high(NG - 1)
            if ln:
                for b in range(2):
                    act.wait_ge(x_stored[b], ONE + 16 * (NG // 2))
            act.wait_ge(fT_stored, ONE + 16 * NG)
            for b in range(2):
                act.wait_ge(v_stored[b], ONE + 16 * (NC // 2))
            act.wait_ge(rf_step, ONE + 5)
            nc.scalar.activation(rowf[:, :, 0:2 * H], rfm[:, :, :, :].rearrange("p c h k -> p c (h k)"), ACT.Exp).then_inc(rf_ready, 1)

        @block.gpsimd
        def _(pool):
            with pool.Fori(0, NC // 2) as t:
                for b in range(2):
                    pool.wait_ge(high_ready, ONE + 2 * t + b + 1)
                    nc.gpsimd.tensor_tensor(vh[b][:, :, :, 1, :], vf[b][:, :, :, :], vh[b][:, :, :, 0, :], ALU.subtract)\
                        .then_inc(low_ready, 1)

        @block.tensor
        def _(pe):
            def group(g, r, b):
                for c in range(G):
                    if ln:
                        pe.wait_ge(x_ready, ONE + G * g + c + 1)
                    elif c == 0:
                        pe.wait_ge(x_loaded[b], ONE + LOADS * r + LOADS)
                    if c < 2:
                        pe.wait_ge(xT_ready, ONE + G * g)
                    else:
                        pe.wait_ge(xT_ready, ONE + G * g + c - 1)
                    for kc in range(KC):
                        last = nc.tensor.transpose(pT[c % 2][:, kc, :], x[:, b, c, kc * P:(kc + 1) * P], ident[:, :])
                    last.then_inc(turned[b], 1)
                pe.wait_ge(f_copied, ONE + 4 * g)
                for c in range(G):
                    pe.wait_ge(xT_ready, ONE + G * g + c + 1)
                    for kc in range(KC):
                        last = nc.tensor.matmul(pF[:, c, :], xT[:, c, kc, :], wa[:, kc, :], start=kc == 0, stop=kc == KC - 1)
                last.then_inc(f_done, 1)
                for c in range(G):
                    if c == 0:
                        pe.wait_ge(v_ready, ONE + 3 * G * g)
                    for kc in range(KC):
                        last = nc.tensor.matmul(pW[c][:, :], xT[:, c, kc, :], w_sb[:, kc, :],
                                                start=kc == 0, stop=kc == KC - 1)
                    last.then_inc(wx_done, 1)
                pe.wait_ge(f_copied, ONE + 4 * g + 1)
                pe.wait_ge(fT_copied, ONE + g)
                for c in range(G):
                    last = nc.tensor.transpose(pFT_f[:, c, :], fst[:, c, :], ident[:, :])
                last.then_inc(fT_done, 1)

            pe.wait_ge(wa_step, ONE + 4)
            with pe.Fori(0, NG // 2) as r:
                for b in range(2):
                    group(2 * r + b, r, b)
    free_semaphores(nc, sems)


def attend(nc, lay, number, mask, mask_dram, v_dram, f1_dram, attn, cols, ident_bf):
    H, D, VW, IB, NIB, CB, CPB = lay.H, lay.D, lay.VW, lay.IB, lay.NIB, lay.CB, lay.CPB
    f12, beta, ndelta, rowf = cols
    D1 = D + 1
    NB = CB // CPB
    BLOCKS = H * NIB
    U = 4
    ROUNDS = NC // U
    ctx = ExitStack()
    with ctx:
        def sb(name, shape, dt):
            return ctx.enter_context(nc.sbuf_tensor(f"{name}_{number}", shape, dt))

        sems = []

        def sem(name):
            sems.append(nc.alloc_semaphore(f"{name}_{number}"))
            return sems[-1]

        val = sb("val", [P, NC, VW], F16)
        f1b = [sb(f"f1b{b}", [P, 1, IB], F32) for b in range(2)]
        odd = [sb(f"odd{k}", [P, IB], BF16) for k in range(U // 2)]
        y = [sb(f"y{u}", [P, IB], BF16) for u in range(U)]
        S = [sb(f"S{b}", [P, IB], BF16) for b in range(2)]
        T = [sb(f"T{b}", [P, IB], BF16) for b in range(2)]
        part = sb("part", [P, 2, NB, CPB, D1], F32)
        res = part[:, 1, :, :, :].rearrange("p n q d -> p (n q d)")[:, 0:CB * D]
        rden = sb("rden", [P, NB, CPB], F32)
        acc = ctx.enter_context(nc.psum_tensor(f"acc_{number}", [P, NB, 512], F32))

        v_loaded, v_last_loaded = sem("val_loaded"), sem("val_last_loaded")
        f1_loaded = [sem(f"f1_loaded{b}") for b in range(2)]
        odd_loaded = [sem(f"odd_loaded{k}") for k in range(U // 2)]
        y_ready = [sem(f"y_ready{u}") for u in range(U)]
        z_ready = [sem(f"z_ready{u}") for u in range(U)]
        s_ready = [sem(f"s_ready{u}") for u in range(U)]
        t_ready = [sem(f"t_ready{u}") for u in range(U)]
        st_used = [sem(f"st_used{u}") for u in range(U)]
        acc_read, sum_step, res_ready, res_stored = sem("acc_read"), sem("sum_step"), sem("res_ready"), sem("res_stored")
        start_at_one(nc, sems)
        block = ctx.enter_context(nc.Block())

        v_v = v_dram[:, 0:H * VW].rearrange("(q c p) m -> q p c m", c=U, p=P)
        out_v = attn.rearrange("(b c p) f -> b p c f", c=CB, p=P)

        @block.sync
        def _(sp):
            def f1_load(h, ib, b):
                sp.dma_start(f1b[b][:, :, :], f1_dram[bass.ds(h, 1), ib * IB:(ib + 1) * IB].partition_broadcast(P))\
                    .then_inc(f1_loaded[b], 16)

            def v_load(h, q):
                sp.dma_start(val[:, bass.ds(q * U, U), :], v_v[q][:, :, bass.ds(h * VW, VW)])\
                    .then_inc(v_last_loaded if isinstance(q, int) and q == ROUNDS - 1 else v_loaded, 16)

            def odd_loads(m, ib, jq):
                for k in range(U // 2):
                    sp.wait_ge(z_ready[2 * k + 1], ONE + m * ROUNDS + jq)
                    sp.dma_start(odd[k][:, :], mask_dram[2 * jq + k][:, ib * IB:(ib + 1) * IB])\
                        .then_inc(odd_loaded[k], 16)

            def next_values(h, m, q):
                for u in range(U):
                    sp.wait_ge(st_used[u], ONE + m * ROUNDS + q + 1)
                v_load(h + 1, q)

            def store(h, ib, m):
                sp.wait_ge(res_ready, ONE + m + 1)
                sp.dma_start(out_v[ib][:, :, bass.ds(h * D, D)], res.rearrange("p (c d) -> p c d", c=CB)).then_inc(res_stored, 16)

            def head(h, first, last):
                for ib in range(NIB):
                    m = h * NIB + ib
                    odd_loads(m, ib, 1)
                    if not (first and ib == 0):
                        if ib == 0:
                            next_values(h - 1, m - 1, ROUNDS - 1)
                            store(h - 1, NIB - 1, m - 1)
                        else:
                            store(h, ib - 1, m - 1)
                        if not (last and ib == NIB - 1):
                            for u in range(U):
                                sp.wait_ge(y_ready[u], ONE + ROUNDS * m)
                            if ib == NIB - 1:
                                f1_load(h + 1, 0, 0)
                            else:
                                f1_load(h, ib + 1, (ib + 1) % 2)
                    with sp.Fori(2, ROUNDS) as jq:
                        odd_loads(m, ib, jq)
                        if ib == NIB - 1 and not last:
                            next_values(h, m, jq - 2)
                    if not (last and ib == NIB - 1):
                        odd_loads(m + 1, (ib + 1) % NIB, 0)
                        if ib == NIB - 1:
                            next_values(h, m, ROUNDS - 2)

            f1_load(0, 0, 0)
            odd_loads(0, 0, 0)
            for q in range(ROUNDS):
                v_load(0, q)
            f1_load(0, 1, 1)
            head(0, True, False)
            with sp.Fori(1, H - 1) as h:
                head(h, False, False)
            head(H - 1, False, True)
            store(H - 1, NIB - 1, BLOCKS - 1)
            sp.wait_ge(res_stored, ONE + 16 * BLOCKS)

        @block.scalar
        def _(act):
            AHEAD = 2

            def sign(m, s, jq, u):
                h, R = m // NIB, m * ROUNDS + jq
                act.wait_ge(s_ready[u], ONE + R)
                act.wait_ge(t_ready[u], ONE + R)
                nc.scalar.activation(y[u][:, :], f1b[s][:, 0, :], ACT.Sign, bias=f12[:, U * jq + u, bass.ds(H + h, 1)])\
                    .then_inc(y_ready[u], 1)

            def t_part(m, jq):
                h, R, u = m // NIB, m * ROUNDS + jq, U - 1
                act.wait_ge(z_ready[u], ONE + R + 1)
                act.wait_ge(st_used[u - 2], ONE + R + 1)
                nc.scalar.activation(T[u % 2][:, :], y[u][:, :], ACT.Relu, scale=ndelta[:, U * jq + u, bass.ds(h, 1)])\
                    .then_inc(t_ready[u], 1)

            def rounds(m, s, last):
                for u in range(AHEAD, U):
                    sign(m, s, 0, u)
                with act.Fori(1, ROUNDS) as jq:
                    for u in range(AHEAD):
                        sign(m, s, jq, u)
                    t_part(m, jq - 1)
                    for u in range(AHEAD, U):
                        sign(m, s, jq, u)
                if not last:
                    act.wait_ge(f1_loaded[1 - s], ONE + 16 * ((m + 1) // 2) + 16)
                    for u in range(AHEAD):
                        sign(m + 1, 1 - s, 0, u)
                t_part(m, ROUNDS - 1)

            act.wait_ge(f1_loaded[0], ONE + 16)
            for u in range(AHEAD):
                sign(0, 0, 0, u)
            with act.Fori(0, BLOCKS // 2 - 1) as m2:
                for s in range(2):
                    rounds(2 * m2 + s, s, False)
            for s in range(2):
                rounds(BLOCKS - 2 + s, s, s == 1)

        @block.vector
        def _(dve):
            def masked(m, jq, u):
                ib, R = m % NIB, m * ROUNDS + jq
                if u % 2:
                    dve.wait_ge(odd_loaded[u // 2], ONE + 16 * R + 16)
                    chunk = odd[u // 2][:, :]
                else:
                    chunk = mask[:, 2 * jq + u // 2, bass.ds(ib * IB, IB)]
                dve.wait_ge(y_ready[u], ONE + R + 1)
                nc.vector.tensor_tensor(y[u][:, :], y[u][:, :], chunk, ALU.mult).then_inc(z_ready[u], 1)

            def matrices(m, jq, u):
                h, R = m // NIB, m * ROUNDS + jq
                dve.wait_ge(z_ready[u], ONE + R + 1)
                dve.wait_ge(st_used[(u + 2) % U], ONE + R + u // 2)
                nc.vector.tensor_scalar(S[u % 2][:, :], y[u][:, :], 0.0, beta[:, U * jq + u, 0, bass.ds(h, 1)],
                                        ALU.max, ALU.mult).then_inc(s_ready[u], 1)
                if u < U - 1:
                    nc.vector.tensor_scalar(T[u % 2][:, :], y[u][:, :], 0.0, ndelta[:, U * jq + u, bass.ds(h, 1)],
                                            ALU.min, ALU.mult).then_inc(t_ready[u], 1)

            def half(m, jq, k, follows):
                for u in (2 * k, 2 * k + 1):
                    if u < U - 1:
                        masked(m, jq, u + 1)
                    elif follows is not None:
                        masked(*follows, 0)
                    matrices(m, jq, u)

            def normalise(m):
                h, ib = m // NIB, m % NIB
                for u in range(U):
                    dve.wait_ge(st_used[u], ONE + ROUNDS * m + ROUNDS)
                dve.wait_ge(sum_step, ONE + 2 * m)
                dve.wait_ge(res_stored, ONE + 16 * m)
                for k in range(2):
                    nc.vector.tensor_tensor(part[:, k, :, :, :],
                                            acc[:, :, 0:CPB * 2 * D1].rearrange("p n (q k d) -> p k n q d", q=CPB, k=2)[:, k],
                                            rowf[:, bass.ds(ib * CB, CB), bass.ds(2 * h + k, 1)]
                                            .rearrange("p (n q) o -> p n q o", q=CPB)
                                            .to_broadcast([P, NB, CPB, D1]), ALU.mult).then_inc(acc_read, 1)
                dve.wait_ge(acc_read, ONE + 2 * m + 2)
                nc.vector.tensor_tensor(part[:, 0, :, :, :], part[:, 0, :, :, :], part[:, 1, :, :, :], ALU.add)\
                    .then_inc(sum_step, 1)
                dve.wait_ge(sum_step, ONE + 2 * m + 1)
                nc.vector.reciprocal(rden[:, :, :], part[:, 0, :, :, D]).then_inc(sum_step, 1)
                dve.wait_ge(sum_step, ONE + 2 * m + 2)
                nc.vector.tensor_tensor(res.rearrange("p (n q d) -> p n q d", n=NB, q=CPB), part[:, 0, :, :, 0:D],
                                        rden[:, :, :].rearrange("p n (q o) -> p n q o", o=1)
                                        .to_broadcast([P, NB, CPB, D]), ALU.mult).then_inc(res_ready, 1)

            def rest_of(m, follows):
                half(m, 0, 1, (m, 1))
                with dve.Fori(1, ROUNDS - 1) as jq:
                    half(m, jq, 0, None)
                    half(m, jq, 1, (m, jq + 1))
                half(m, ROUNDS - 1, 0, None)
                half(m, ROUNDS - 1, 1, follows)

            masked(0, 0, 0)
            half(0, 0, 0, None)
            with dve.Fori(0, BLOCKS - 1) as m:
                rest_of(m, (m + 1, 0))
                half(m + 1, 0, 0, None)
                normalise(m)
            rest_of(BLOCKS - 1, None)
            normalise(BLOCKS - 1)

        @block.tensor
        def _(pe):
            def sums(m, jq):
                R = m * ROUNDS + jq
                for u in range(U):
                    for k, (M, ready) in enumerate(((S, s_ready), (T, t_ready))):
                        pe.wait_ge(ready[u], ONE + R + 1)
                        for c in range(CB):
                            at = (2 * (c % CPB) + k) * D1
                            for part_of in range(2):
                                v0 = (2 * k + part_of) * D1
                                last = nc.tensor.matmul(acc[:, c // CPB, at:at + D1], M[u % 2][:, c * P:(c + 1) * P],
                                                        val[:, U * jq + u, v0:v0 + D1], start=False, stop=False,
                                                        skip_group_check=True)
                    last.then_inc(st_used[u], 1)

            with pe.Fori(0, BLOCKS) as m:
                pe.wait_ge(acc_read, ONE + 2 * m)
                pe.wait_ge(v_loaded, ONE + 16 * (ROUNDS - 1) * (m // NIB + 1))
                for n in range(NB):
                    nc.tensor.matmul(acc[:, n, 510:512], ident_bf[:, :], ident_bf[:, 0:2], start=True, stop=True,
                                     skip_group_check=True)
                with pe.Fori(0, ROUNDS - 1) as jq:
                    sums(m, jq)
                pe.wait_ge(v_last_loaded, ONE + 16 * (m // NIB + 1))
                sums(m, ROUNDS - 1)
    free_semaphores(nc, sems)


def last_layer(nc, x_in, attn, w_self, w_neigh, mask, mask_dram, y_dram, x_dram, out, ident, ident_bf):
    number = 3
    G = 4
    NG = NC // G
    ctx = ExitStack()
    with ctx:
        def sb(name, shape, dt):
            return ctx.enter_context(nc.sbuf_tensor(f"{name}_{number}", shape, dt))

        r_bc = sb("r_bc", [P, F], F32)
        x0 = sb("x0", [P, NC], F32)
        s_col = sb("s_col", [P, NC], F32)
        self_product(nc, G, NG, x_in, attn, w_self, w_neigh, y_dram, x_dram, ident, r_bc, x0)
        neighbour_sums(nc, mask, mask_dram, ident_bf, x0, s_col)
        combine(nc, G, NG, y_dram, x_dram, r_bc, s_col, out)


def self_product(nc, G, NG, x_in, attn, w_self, w_neigh, y_dram, x_dram, ident, r_bc, x0):
    ctx = ExitStack()
    with ctx:
        def sb(name, shape, dt):
            return ctx.enter_context(nc.sbuf_tensor(f"{name}_3a", shape, dt))

        def ps(name, shape, dt):
            return ctx.enter_context(nc.psum_tensor(f"{name}_3a", shape, dt))

        sems = []

        def sem(name):
            sems.append(nc.alloc_semaphore(f"{name}_3a"))
            return sems[-1]

        w_rows = sb("w_rows", [P, 2, KC, F], F32)
        wT = sb("wT", [P, KC, F], F32)
        rn = sb("rn", [P, KC], F32)
        rn_b = sb("rn_b", [P, KC, P], F32)
        x = sb("x", [P, 2, G, F], F32)
        o = sb("o", [P, 2, G, F], F32)
        neg = sb("neg", [P, G, F], F32)
        xT = sb("xT", [P, 2, KC, P], F32)
        ys = sb("ys", [P, 2, F], F32)
        norm = Norm(nc, sb, sem, G)
        eluw = {k: sem(f"elu_{k}") for k in ("neg", "exp", "added")}
        pT = [ps(f"pT{b}", [P, KC, P], F32) for b in range(2)]
        pW = [ps(f"pW{b}", [P, F], F32) for b in range(2)]
        w_loaded, rn_ready, rnb_ready, r_done, r_copied = (sem(n) for n in ("w_loaded", "rn_ready", "rnb_ready", "r_done", "r_copied"))
        w_turned, wT_ready = sem("w_turned"), sem("wT_ready")
        x_loaded = [sem(f"x_loaded{b}") for b in range(2)]
        x_stored = [sem(f"x_stored{b}") for b in range(2)]
        x0_ready = sem("x0_ready")
        turned = [sem(f"turned{b}") for b in range(2)]
        xT_ready, y_done, y_copied = sem("xT_ready"), sem("y_done"), sem("y_copied")
        y_stored = [sem(f"y_stored{b}") for b in range(2)]
        start_at_one(nc, sems)
        block = ctx.enter_context(nc.Block())
        x_v = x_in.rearrange("(g c p) f -> g p c f", c=G, p=P)
        o_v = attn.rearrange("(g c p) f -> g p c f", c=G, p=P)
        xo_v = x_dram.rearrange("(g c p) f -> g p c f", c=G, p=P)
        y_v = y_dram.rearrange("(c p) f -> c p f", p=P)

        @block.sync
        def _(sp):
            for k, w in enumerate((w_self, w_neigh)):
                sp.dma_start(w_rows[:, k, :, :], w.rearrange("(c p) f -> p c f", p=P)).then_inc(w_loaded, 16)
            with sp.Fori(0, NG // 2) as r:
                for b in range(2):
                    sp.wait_ge(turned[b], ONE + G * r)
                    sp.wait_ge(x_stored[b], ONE + 16 * r)
                    sp.dma_start(x[:, b, :, :], x_v[2 * r + b]).then_inc(x_loaded[b], 16)
                    sp.dma_start(o[:, b, :, :], o_v[2 * r + b]).then_inc(x_loaded[b], 16)

        @block.vector
        def _(dve):
            dve.wait_ge(w_loaded, ONE + 32)
            nc.vector.tensor_reduce(rn[:, :], w_rows[:, 1, :, :], AX.X, ALU.add).then_inc(rn_ready, 1)
            dve.wait_ge(rn_ready, ONE + 1)
            nc.vector.tensor_copy(rn_b[:, :, :], rn[:, :].rearrange("p (c o) -> p c o", o=1).to_broadcast([P, KC, P]))\
                .then_inc(rnb_ready, 1)
            with dve.Fori(0, NG // 2) as r:
                for b in range(2):
                    g = 2 * r + b
                    dve.wait_ge(x_loaded[b], ONE + 32 * r + 32)
                    add_elu(nc, dve, g, x[:, b, :, :], o[:, b, :, :], neg, eluw)
                    dve.wait_ge(eluw["added"], ONE + 2 * g + 2)
                    norm.rows(dve, g, x, b)
                    dve.wait_ge(norm.ready, ONE + G * g + G)
                    nc.vector.tensor_copy(x0[:, bass.ds(G * g, G)], x[:, b, :, 0]).then_inc(x0_ready, 1)

        @block.scalar
        def _(act):
            def exps(g):
                act.wait_ge(eluw["neg"], ONE + g + 1)
                nc.scalar.activation(neg[:, :, :], neg[:, :, :], ACT.Exp).then_inc(eluw["exp"], 1)
                norm.rsqrt(act, g)

            def products(g, r, b):
                act.wait_ge(x0_ready, ONE + g + 1)
                act.dma_start(xo_v[g], x[:, b, :, :]).then_inc(x_stored[b], 16)
                for c in range(G):
                    act.wait_ge(turned[b], ONE + G * r + c + 1)
                    act.wait_ge(y_done, ONE + G * g + c - 1 if c else ONE + G * g)
                    nc.scalar.activation(xT[:, c % 2, :, :], pT[c % 2][:, :, :], ACT.Copy).then_inc(xT_ready, 1)
                    act.wait_ge(y_done, ONE + G * g + c + 1)
                    act.wait_ge(y_stored[c % 2], ONE + 16 * (2 * g + c // 2))
                    nc.scalar.activation(ys[:, c % 2, :], pW[c % 2][:, :], ACT.Copy).then_inc(y_copied, 1)
                    act.wait_ge(y_copied, ONE + G * g + c + 1)
                    act.dma_start(y_v[G * g + c], ys[:, c % 2, :]).then_inc(y_stored[c % 2], 16)

            for c in range(KC):
                act.wait_ge(w_turned, ONE + c + 1)
                nc.scalar.activation(wT[:, c, :], pT[c % 2][:, :, :].rearrange("p c f -> p (c f)"), ACT.Copy).then_inc(wT_ready, 1)
            act.wait_ge(r_done, ONE + 1)
            nc.scalar.activation(r_bc[:, :], pW[0][:, :], ACT.Copy).then_inc(r_copied, 1)
            exps(0)
            with act.Fori(0, NG // 2 - 1) as r:
                exps(2 * r + 1)
                products(2 * r, r, 0)
                exps(2 * r + 2)
                products(2 * r + 1, r, 1)
            exps(NG - 1)
            products(NG - 2, NG // 2 - 1, 0)
            products(NG - 1, NG // 2 - 1, 1)
            for b in range(2):
                act.wait_ge(y_stored[b], ONE + 16 * (NC // 2))
                act.wait_ge(x_stored[b], ONE + 16 * (NG // 2))

        @block.tensor
        def _(pe):
            pe.wait_ge(w_loaded, ONE + 32)
            for c in range(KC):
                if c >= 2:
                    pe.wait_ge(wT_ready, ONE + c - 1)
                for k in range(KC):
                    last = nc.tensor.transpose(pT[c % 2][:, k, :], w_rows[:, 0, k, c * P:(c + 1) * P], ident[:, :])
                last.then_inc(w_turned, 1)
            pe.wait_ge(rnb_ready, ONE + 1)
            for c in range(KC):
                last = nc.tensor.matmul(pW[0][:, c * P:(c + 1) * P], rn_b[:, c, :], ident[:, :], start=True, stop=True)
            last.then_inc(r_done, 1)
            pe.wait_ge(r_copied, ONE + 1)
            pe.wait_ge(wT_ready, ONE + KC)
            with pe.Fori(0, NG // 2) as r:
                for b in range(2):
                    g = 2 * r + b
                    for c in range(G):
                        pe.wait_ge(norm.ready, ONE + G * g + c + 1)
                        if c < 2:
                            pe.wait_ge(xT_ready, ONE + G * g)
                        else:
                            pe.wait_ge(xT_ready, ONE + G * g + c - 1)
                        for kc in range(KC):
                            last = nc.tensor.transpose(pT[c % 2][:, kc, :], x[:, b, c, kc * P:(kc + 1) * P], ident[:, :])
                        last.then_inc(turned[b], 1)
                        pe.wait_ge(xT_ready, ONE + G * g + c + 1)
                        if c < 2:
                            pe.wait_ge(y_copied, ONE + G * g)
                        else:
                            pe.wait_ge(y_copied, ONE + G * g + c - 1)
                        for kc in range(KC):
                            last = nc.tensor.matmul(pW[c % 2][:, :], xT[:, c % 2, kc, :], wT[:, kc, :],
                                                    start=kc == 0, stop=kc == KC - 1)
                        last.then_inc(y_done, 1)
    free_semaphores(nc, sems)


def neighbour_sums(nc, mask, mask_dram, ident_bf, x0, s_col):
    ctx = ExitStack()
    with ctx:
        def sb(name, shape, dt):
            return ctx.enter_context(nc.sbuf_tensor(f"{name}_3b", shape, dt))

        sems = []

        def sem(name):
            sems.append(nc.alloc_semaphore(f"{name}_3b"))
            return sems[-1]

        parts = sb("parts", [P, NC, 3], BF16)
        rest = sb("rest", [P, 2, NC], F32)
        odd = [sb(f"odd{b}", [P, N], BF16) for b in range(2)]
        acc = ctx.enter_context(nc.psum_tensor("acc_3b", [P, NC, 16], F32))
        split, summed = sem("split"), sem("summed")
        odd_loaded = [sem(f"odd_loaded{b}") for b in range(2)]
        used = [sem(f"used{b}") for b in range(2)]
        start_at_one(nc, sems)
        block = ctx.enter_context(nc.Block())

        @block.sync
        def _(sp):
            with sp.Fori(0, NC // 4) as t:
                for b in range(2):
                    sp.wait_ge(used[b], ONE + t)
                    sp.dma_start(odd[b][:, :], mask_dram[2 * t + b]).then_inc(odd_loaded[b], 16)

        @block.vector
        def _(dve):
            nc.vector.tensor_copy(parts[:, :, 0], x0[:, :]).then_inc(split, 1)
            dve.wait_ge(split, ONE + 1)
            nc.vector.tensor_tensor(rest[:, 0, :], x0[:, :], parts[:, :, 0], ALU.subtract).then_inc(split, 1)
            dve.wait_ge(split, ONE + 2)
            nc.vector.tensor_copy(parts[:, :, 1], rest[:, 0, :]).then_inc(split, 1)
            dve.wait_ge(split, ONE + 3)
            nc.vector.tensor_tensor(rest[:, 1, :], rest[:, 0, :], parts[:, :, 1], ALU.subtract).then_inc(split, 1)
            dve.wait_ge(split, ONE + 4)
            nc.vector.tensor_copy(parts[:, :, 2], rest[:, 1, :]).then_inc(split, 1)
            for b in range(2):
                dve.wait_ge(used[b], ONE + NC // 4)
            nc.vector.tensor_reduce(s_col[:, :], acc[:, :, 0:3], AX.X, ALU.add).then_inc(summed, 1)

        @block.tensor
        def _(pe):
            def chunk(stationary, j):
                for c in range(NC):
                    last = nc.tensor.matmul(acc[:, c, 0:3], stationary[:, c * P:(c + 1) * P], parts[:, j, :],
                                            start=False, stop=False, skip_group_check=True)
                return last

            nc.tensor.matmul(acc[:, NC - 1, 14:16], ident_bf[:, :], ident_bf[:, 0:2], start=True, stop=True, skip_group_check=True)
            pe.wait_ge(split, ONE + 5)
            with pe.Fori(0, NC // 4) as t:
                for b in range(2):
                    chunk(mask[:, 2 * t + b, :], 4 * t + 2 * b)
                    pe.wait_ge(odd_loaded[b], ONE + 16 * t + 16)
                    chunk(odd[b], 4 * t + 2 * b + 1).then_inc(used[b], 1)
    free_semaphores(nc, sems)


def combine(nc, G, NG, y_dram, x_dram, r_bc, s_col, out):
    ctx = ExitStack()
    with ctx:
        def sb(name, shape, dt):
            return ctx.enter_context(nc.sbuf_tensor(f"{name}_3c", shape, dt))

        sems = []

        def sem(name):
            sems.append(nc.alloc_semaphore(f"{name}_3c"))
            return sems[-1]

        x = sb("x", [P, 2, G, F], F32)
        y = sb("y", [P, 2, G, F], F32)
        norm = Norm(nc, sb, sem, G)
        loaded = [sem(f"loaded{b}") for b in range(2)]
        stored = [sem(f"stored{b}") for b in range(2)]
        y_step, added = sem("y_step"), sem("added")
        start_at_one(nc, sems)
        block = ctx.enter_context(nc.Block())
        x_v = x_dram.rearrange("(g c p) f -> g p c f", c=G, p=P)
        y_v = y_dram.rearrange("(g c p) f -> g p c f", c=G, p=P)
        out_v = out.rearrange("(g c p) f -> g p c f", c=G, p=P)

        @block.sync
        def _(sp):
            with sp.Fori(0, NG // 2) as r:
                for b in range(2):
                    sp.wait_ge(stored[b], ONE + 16 * r)
                    sp.dma_start(x[:, b, :, :], x_v[2 * r + b]).then_inc(loaded[b], 16)
                    sp.dma_start(y[:, b, :, :], y_v[2 * r + b]).then_inc(loaded[b], 16)

        @block.scalar
        def _(act):
            with act.Fori(0, NG // 2) as r:
                for b in range(2):
                    g = 2 * r + b
                    norm.rsqrt(act, g)
                    act.wait_ge(norm.ready, ONE + G * g + G)
                    act.dma_start(out_v[g], x[:, b, :, :]).then_inc(stored[b], 16)
            for b in range(2):
                act.wait_ge(stored[b], ONE + 16 * (NG // 2))

        @block.vector
        def _(dve):
            with dve.Fori(0, NG // 2) as r:
                for b in range(2):
                    g = 2 * r + b
                    dve.wait_ge(loaded[b], ONE + 32 * r + 32)
                    for c in range(G):
                        nc.vector.scalar_tensor_tensor(y[:, b, c, :], r_bc[:, :], s_col[:, bass.ds(G * g + c, 1)],
                                                       y[:, b, c, :], ALU.mult, ALU.add).then_inc(y_step, 1)
                    dve.wait_ge(y_step, ONE + G * g + G)
                    nc.vector.scalar_tensor_tensor(x[:, b, :, :], y[:, b, :, :], 0.0, x[:, b, :, :], ALU.max, ALU.add)\
                        .then_inc(added, 1)
                    dve.wait_ge(added, ONE + g + 1)
                    norm.rows(dve, g, x, b)
    free_semaphores(nc, sems)


def gat_kernel(nc, x, adj, W0, a1, a2, W1, a, W2, a_l, a_r, w_self, w_neigh, out):
    def dram(name, shape, dt):
        return nc.dram_tensor(name, shape, dt, kind="Internal").ap()

    f1_dram = dram("f1_rows", (8, N), F32)
    v_dram = dram("values", (N, 8 * 4 * 65), F16)
    attn = dram("attended", (N, F), F32)
    mask_dram = dram("mask_odd", (NC // 2, P, N), BF16)
    y_dram = dram("self_products", (N, F), F32)
    rows = [dram(f"rows{k}", (N, F), F32) for k in range(2)]

    ctx = ExitStack()
    with ctx:
        def sb(name, shape, dt):
            return ctx.enter_context(nc.sbuf_tensor(name, shape, dt))

        mask = sb("mask", [P, NC // 2, N], BF16)
        f12 = sb("f12", [P, NC, 16], F32)
        beta = sb("beta", [P, NC, 2, 8], BF16)
        rowf = sb("rowf", [P, NC, 16], F32)
        ndelta = sb("ndelta", [P, NC, 8], F32)
        ident = sb("ident", [P, P], F32)
        ident_bf = sb("ident_bf", [P, P], BF16)
        cols = (f12, beta, ndelta, rowf)
        made = ctx.enter_context(nc.semaphore("ident_made"))
        with nc.Block() as block:
            @block.gpsimd
            def _(pool):
                nc.gpsimd.memset(ident[:, :], 0.0).then_inc(made, 1)
                nc.gpsimd.memset(ident_bf[:, :], 0.0).then_inc(made, 1)
                pool.wait_ge(made, 2)
                for m in (ident, ident_bf):
                    nc.gpsimd.affine_select(out=m[:, :], in_=m[:, :], compare_op=ALU.not_equal, fill=1.0, base=0,
                                            pattern=[[-1, P]], channel_multiplier=1).then_inc(made, 1)
                pool.wait_ge(made, 4)

        eight, four = Layer(8), Layer(4)
        load_adjacency(nc, adj, mask, mask_dram, ident_bf)
        w0 = [W0[:, k * P:(k + 1) * P, :].rearrange("h k o -> k h o") for k in range(KC)]
        w1 = [W1[k * P:(k + 1) * P, :] for k in range(KC)]
        w2 = [W2[k * P:(k + 1) * P, :] for k in range(KC)]
        flat = [a1.rearrange("h o -> (h o)"), a2.rearrange("h o -> (h o)")]
        prepare(nc, eight, 0, x, None, False, w0, *flat, None, v_dram, f1_dram, cols, ident)
        attend(nc, eight, 0, mask, mask_dram, v_dram, f1_dram, attn, cols, ident_bf)
        flat = [a[0, :, k * 64:(k + 1) * 64] for k in range(2)]
        prepare(nc, eight, 1, x, attn, False, w1, *flat, rows[0], v_dram, f1_dram, cols, ident)
        attend(nc, eight, 1, mask, mask_dram, v_dram, f1_dram, attn, cols, ident_bf)
        flat = [m.rearrange("h o -> (h o)") for m in (a_l, a_r)]
        prepare(nc, four, 2, rows[0], attn, True, w2, *flat, rows[1], v_dram, f1_dram, cols, ident)
        attend(nc, four, 2, mask, mask_dram, v_dram, f1_dram, attn, cols, ident_bf)
        last_layer(nc, rows[1], attn, w_self, w_neigh, mask, mask_dram, y_dram, rows[0], out, ident, ident_bf)


_INS = ['x', 'adj', 'L0_gnn_W', 'L0_gnn_a1', 'L0_gnn_a2', 'L1_gnn_W', 'L1_gnn_a', 'L2_gnn_W', 'L2_gnn_a_l', 'L2_gnn_a_r',
        'L3_gnn_w_self', 'L3_gnn_w_neigh']


def kernel(**inputs):
    import numpy as np
    import concourse.bacc as bacc
    from concourse.bass_utils import run_bass_kernel_spmd

    nc = bacc.Bacc("TRN2", target_bir_lowering=False, num_devices=1,
                   dynamic_dma_scratch_size=4096)
    arrays, args = {}, []
    for name in _INS:
        a = np.ascontiguousarray(inputs[name])
        arrays[f"in_{name}"] = a
        args.append(nc.dram_tensor(f"in_{name}", a.shape, mybir.dt.from_np(a.dtype), kind="ExternalInput").ap())
    args.append(nc.dram_tensor("out_0", (N, F), F32, kind="ExternalOutput").ap())
    gat_kernel(nc, *args)
    r = run_bass_kernel_spmd(nc, [arrays], core_ids=[0])
    return r.results[0]["out_0"]
```

```python
import concourse.bass as bass
from concourse import mybir
from contextlib import ExitStack
import math

F32 = mybir.dt.float32
BF16 = mybir.dt.bfloat16
F16 = mybir.dt.float16
I32 = mybir.dt.int32
ALU = mybir.AluOpType
ACT = mybir.ActivationFunctionType
AX = mybir.AxisListType

N = 4096
F = 512
P = 128
NC = N // P
KC = F // P
EPS = 1e-5
SLOPE = 0.2
LN2 = math.log(2.0)
VSCALE = 64.0
ROUNDER = 1.5 * 2.0 ** 23
ONE = 1
TINY = 1e-30


def start_at_one(nc, sems):
    for s in sems:
        nc.gpsimd.sem_inc(s, ONE)
    nc.all_engine_barrier()


def free_semaphores(nc, sems):
    nc.clear_and_free_semaphores(sems)
    nc.all_engine_barrier()


class Layer:

    def __init__(self, heads):
        self.H = heads
        self.D = F // heads
        self.VW = 2 * 2 * (self.D + 1)
        self.CPB = min(2, 512 // (2 * (self.D + 1)))
        self.IB = 8 * self.CPB * P
        self.NIB = N // self.IB
        self.CB = self.IB // P


def load_adjacency(nc, adj, mask, mask_dram, ident_bf):
    ctx = ExitStack()
    with ctx:
        raw = [ctx.enter_context(nc.sbuf_tensor(f"adj_raw{b}", [P, N], I32)) for b in range(2)]
        one = [ctx.enter_context(nc.sbuf_tensor(f"adj_one{b}", [P, N], BF16)) for b in range(2)]
        G = 4
        odd = [ctx.enter_context(nc.sbuf_tensor(f"adj_odd{b}", [P, NC // 2, G * P], BF16)) for b in range(2)]
        turned = [[ctx.enter_context(nc.psum_tensor(f"adj_turned{b}{g}", [P, 8, P], BF16)) for g in range(4)]
                  for b in range(2)]
        sems = []

        def sem(name):
            sems.append(nc.alloc_semaphore(name))
            return sems[-1]

        loaded = [sem(f"adj_loaded{b}") for b in range(2)]
        converted = [sem(f"adj_converted{b}") for b in range(2)]
        bank_turned = [sem(f"adj_bank_turned{b}") for b in range(2)]
        kept = [sem(f"adj_kept{b}") for b in range(2)]
        staged = [sem(f"adj_staged{b}") for b in range(2)]
        stored = [sem(f"adj_stored{s}") for s in range(2)]
        start_at_one(nc, sems)
        block = ctx.enter_context(nc.Block())
        dram_v = mask_dram.rearrange("c p (g i) -> g p c i", i=G * P)

        @block.sync
        def _(sp):
            with sp.Fori(0, NC // 2) as t:
                for b in range(2):
                    sp.wait_ge(converted[b], ONE + t)
                    sp.dma_start(raw[b][:, :], adj[bass.ds((2 * t + b) * P, P), :]).then_inc(loaded[b], 16)

        @block.vector
        def _(dve):
            with dve.Fori(0, NC // 2) as t:
                for b in range(2):
                    dve.wait_ge(loaded[b], ONE + 16 * t + 16)
                    dve.wait_ge(bank_turned[b], ONE + 4 * t)
                    nc.vector.tensor_scalar(one[b][:, :], raw[b][:, :], 0.0, None, ALU.is_gt)\
                        .then_inc(converted[b], 1)
                    for g in range(2):
                        dve.wait_ge(bank_turned[b], ONE + 4 * t + g + 1)
                        nc.vector.tensor_copy(mask[:, 8 * g:8 * g + 8, bass.ds((2 * t + b) * P, P)],
                                              turned[b][g][:, :, :]).then_inc(kept[b], 1)

        @block.scalar
        def _(act):
            with act.Fori(0, NC // (2 * G)) as t:
                for s in range(2):
                    act.wait_ge(stored[s], ONE + 16 * t)
                    for c in range(G):
                        b = c % 2
                        for g in range(2, 4):
                            act.wait_ge(bank_turned[b], ONE + 4 * (4 * t + 2 * s + c // 2) + g + 1)
                            nc.scalar.activation(odd[s][:, 8 * (g - 2):8 * (g - 2) + 8, c * P:(c + 1) * P],
                                                 turned[b][g][:, :, :], ACT.Copy).then_inc(staged[b], 1)
                    for b in range(2):
                        act.wait_ge(staged[b], ONE + 2 * (4 * t + 2 * s + 2))
                    act.dma_start(dram_v[2 * t + s], odd[s][:, :, :]).then_inc(stored[s], 16)
            for s in range(2):
                act.wait_ge(stored[s], ONE + 16 * (NC // (2 * G)))

        @block.tensor
        def _(pe):
            with pe.Fori(0, NC // 2) as t:
                for b in range(2):
                    pe.wait_ge(converted[b], ONE + t + 1)
                    pe.wait_ge(kept[b], ONE + 2 * t)
                    pe.wait_ge(staged[b], ONE + 2 * t)
                    for g in range(4):
                        for c in range(8):
                            j = (2 * (8 * (g % 2) + c) + g // 2) * P
                            last = nc.tensor.transpose(turned[b][g][:, c, :], one[b][:, j:j + P], ident_bf[:, :])
                        last.then_inc(bank_turned[b], 1)

    free_semaphores(nc, sems)


class Norm:

    def __init__(self, nc, sb, sem, G):
        self.nc, self.G = nc, G
        self.stats = sb("stats", [P, G, 6], F32)
        self.mt = sb("mt", [P, 5, G], F32)
        self.mean = sb("mean", [P, G], F32)
        self.ve = sb("ve", [P, G], F32)
        self.lnv = sb("lnv", [P, G], F32)
        self.rs0 = sb("rs0", [P, G], F32)
        self.rt = sb("rt", [P, 3, G], F32)
        self.rs = sb("rs", [P, G], F32)
        self.step = sem("norm_step")
        self.STEPS = G + 10
        self.ve_ready, self.ln_done, self.rs0_ready = sem("ve_ready"), sem("ln_done"), sem("rs0_ready")
        self.ready = sem("x_ready")

    def rows(self, dve, g, x, b):
        self.moments(dve, g, x, b)
        self.finish(dve, g, x, b)

    def moments(self, dve, g, x, b):
        nc, G, step, base = self.nc, self.G, self.step, ONE + self.STEPS * g
        st, mt = self.stats, self.mt
        for c in range(G):
            nc.vector.bn_stats(st[:, c, :], x[:, b, c, :]).then_inc(step, 1)
        dve.wait_ge(self.ready, ONE + G * g)
        dve.wait_ge(step, base + G)
        nc.vector.tensor_tensor(mt[:, 0, :], st[:, :, 1], st[:, :, 4], ALU.subtract).then_inc(step, 1)
        nc.vector.tensor_tensor(mt[:, 1, :], st[:, :, 1], st[:, :, 4], ALU.add).then_inc(step, 1)
        nc.vector.tensor_tensor(mt[:, 2, :], st[:, :, 2], st[:, :, 5], ALU.add).then_inc(step, 1)
        dve.wait_ge(step, base + G + 3)
        nc.vector.tensor_tensor(mt[:, 3, :], mt[:, 0, :], mt[:, 0, :], ALU.mult).then_inc(step, 1)
        nc.vector.tensor_scalar(mt[:, 4, :], mt[:, 2, :], 1.0 / F, EPS, ALU.mult, ALU.add).then_inc(step, 1)
        nc.vector.tensor_scalar(self.mean[:, :], mt[:, 1, :], 0.5, None, ALU.mult).then_inc(step, 1)
        dve.wait_ge(step, base + G + 6)
        nc.vector.scalar_tensor_tensor(self.ve[:, :], mt[:, 3, :], 0.25, mt[:, 4, :], ALU.mult, ALU.add).then_inc(self.ve_ready, 1)

    def finish(self, dve, g, x, b):
        nc, G, step, base = self.nc, self.G, self.step, ONE + self.STEPS * g
        dve.wait_ge(self.rs0_ready, ONE + g + 1)
        nc.vector.tensor_tensor(self.rt[:, 0, :], self.rs0[:, :], self.rs0[:, :], ALU.mult).then_inc(step, 1)
        dve.wait_ge(step, base + G + 6 + 1)
        nc.vector.tensor_tensor(self.rt[:, 1, :], self.rt[:, 0, :], self.ve[:, :], ALU.mult).then_inc(step, 1)
        dve.wait_ge(step, base + G + 6 + 2)
        nc.vector.tensor_scalar(self.rt[:, 2, :], self.rt[:, 1, :], -0.5, 1.5, ALU.mult, ALU.add).then_inc(step, 1)
        dve.wait_ge(step, base + G + 6 + 3)
        nc.vector.tensor_tensor(self.rs[:, :], self.rt[:, 2, :], self.rs0[:, :], ALU.mult).then_inc(step, 1)
        dve.wait_ge(step, base + G + 6 + 4)
        for c in range(G):
            nc.vector.tensor_scalar(x[:, b, c, :], x[:, b, c, :], self.mean[:, c:c + 1], self.rs[:, c:c + 1],
                                    ALU.subtract, ALU.mult).then_inc(self.ready, 1)

    def rsqrt(self, act, g):
        act.wait_ge(self.ve_ready, ONE + g + 1)
        self.nc.scalar.activation(self.lnv[:, :], self.ve[:, :], ACT.Ln).then_inc(self.ln_done, 1)
        act.wait_ge(self.ln_done, ONE + g + 1)
        self.nc.scalar.activation(self.rs0[:, :], self.lnv[:, :], ACT.Exp, scale=-0.5).then_inc(self.rs0_ready, 1)


def split_elu(nc, dve, g, xg, og, neg, sems):
    dve.wait_ge(sems["added"], ONE + 2 * g)
    nc.vector.tensor_scalar(neg[:, :, :], og, 0.0, None, ALU.min).then_inc(sems["neg"], 1)
    nc.vector.scalar_tensor_tensor(xg, og, 0.0, xg, ALU.max, ALU.add).then_inc(sems["added"], 1)


def join_elu(nc, dve, g, xg, neg, sems):
    dve.wait_ge(sems["exp"], ONE + g + 1)
    dve.wait_ge(sems["added"], ONE + 2 * g + 1)
    nc.vector.scalar_tensor_tensor(xg, neg[:, :, :], -1.0, xg, ALU.add, ALU.add).then_inc(sems["added"], 1)
    dve.wait_ge(sems["added"], ONE + 2 * g + 2)


def prepare(nc, lay, number, x_in, attn, elu, w, a_src, a_dst, x_out, v_dram, f1_dram, cols, ident):
    H, D = lay.H, lay.D
    f12, beta, ndelta, rowf = cols
    G = 4
    NG = NC // G
    ln = attn is not None
    LOADS = 16 * (2 if ln else 1)
    ctx = ExitStack()
    with ctx:
        def sb(name, shape, dt):
            return ctx.enter_context(nc.sbuf_tensor(f"{name}_{number}", shape, dt))

        def ps(name, shape, dt):
            return ctx.enter_context(nc.psum_tensor(f"{name}_{number}", shape, dt))

        sems = []

        def sem(name):
            sems.append(nc.alloc_semaphore(f"{name}_{number}"))
            return sems[-1]

        w_sb = sb("w_sb", [P, KC, F], F32)
        wa_tmp = sb("wa_tmp", [P, KC, F], F32)
        wa = sb("wa", [P, KC, 2 * H], F32)
        x = sb("x", [P, 2, G, F], F32)
        if ln:
            o = sb("o", [P, 2, G, F], F32)
            neg = wa_tmp
            norm = Norm(nc, sb, sem, G)
            eluw = {k: sem(f"elu_{k}") for k in ("neg", "exp", "added")}
            x_ready = norm.ready
        xT = sb("xT", [P, 2, G, KC, P], F32)
        frows = sb("frows", [2 * H, G * P], F32)
        f1out = sb("f1out", [2 * H, G * P], I32)
        kexp = sb("kexp", [P, NC, 2, H], F32)
        shifted = sb("shifted", [P, G, 2, H], F32)
        f2low = sb("f2low", [P, G, H], F32)
        rem = sb("rem", [P, G, 2, H], F32)
        rho = sb("rho", [P, G, 2, H], F32)
        lnscale = sb("lnscale", [P, 1], F32)
        kmax = sb("kmax", [P, 2 * H], F32)
        khead = sb("khead", [2 * H, 1], F32)
        kspread = sb("kspread", [2 * H, P], F32)
        ktop = sb("ktop", [P, 2 * H], F32)
        dtop = sb("dtop", [P, H], F32)
        vf = [sb(f"vf{b}", [P, H, 2, D + 1], F32) for b in range(2)]
        vh = [sb(f"vh{b}", [P, H, 2, 2, D + 1], F16) for b in range(2)]
        spare = [t[:, :, :, :].rearrange("p h k d -> p (h k d)") for t in vf]
        a_bc = spare[0][:, 0:2 * F].rearrange("p (k f) -> p k f", k=2)
        rfm = spare[1][:, 0:NC * H * 2].rearrange("p (c h k) -> p c h k", c=NC, h=H)
        fdiff = spare[0][:, 0:NC * H].rearrange("p (c h) -> p c h", c=NC)
        pT = [ps(f"pT{b}", [P, KC, P], F32) for b in range(2)]
        pW = [ps(f"pW{c}", [P, F], F32) for c in range(G)]
        pR = ps("pR", [P, G * P], F32)[0:2 * H, :]
        pC = ps("pC", [P, G, P], F32)[:, :, 0:2 * H]

        w_loaded, a_loaded = sem("w_loaded"), sem("a_loaded")
        wa_step = sem("wa_step")
        x_loaded = [sem(f"x_loaded{b}") for b in range(2)]
        x_stored = [sem(f"x_stored{b}") for b in range(2)]
        turned = [sem(f"turned{b}") for b in range(2)]
        xT_ready = sem("xT_ready")
        pR_done, frows_ready, f1_ready, f1_stored = sem("pR_done"), sem("frows_ready"), sem("f1_ready"), sem("f1_stored")
        pC_done, cols_ready, rho_step = sem("pC_done"), sem("cols_ready"), sem("rho_step")
        wx_done = sem("wx_done")
        v_ready = [sem(f"v_ready{c}") for c in range(G)]
        high_ready = [sem(f"high_ready{b}") for b in range(2)]
        low_ready = [sem(f"low_ready{b}") for b in range(2)]
        v_stored = [sem(f"v_stored{b}") for b in range(2)]
        rem_ready, rho_ready = sem("rem_ready"), sem("rho_ready")
        k_step, k_turned, k_spread, beta_ready = sem("k_step"), sem("k_turned"), sem("k_spread"), sem("beta_ready")
        rf_step, rf_ready = sem("rf_step"), sem("rf_ready")
        start_at_one(nc, sems)
        block = ctx.enter_context(nc.Block())

        x_v = x_in.rearrange("(g c p) f -> g p c f", c=G, p=P)
        o_v = attn.rearrange("(g c p) f -> g p c f", c=G, p=P) if ln else None
        xo_v = x_out.rearrange("(g c p) f -> g p c f", c=G, p=P) if ln else None
        f1_v = f1_dram[0:H, :].rearrange("h (g i) -> g h i", i=G * P)
        v_v = v_dram[:, 0:H * lay.VW].rearrange("(c p) m -> c p m", p=P)

        def later(r, b, k):
            return r + (b + k) // 2, (b + k) % 2

        @block.sync
        def _(sp):
            def load(r, b):
                sp.dma_start(x[:, b, :, :], x_v[2 * r + b]).then_inc(x_loaded[b], 16)
                if ln:
                    sp.dma_start(o[:, b, :, :], o_v[2 * r + b]).then_inc(x_loaded[b], 16)

            def reload(r, b):
                sp.wait_ge(turned[b], ONE + G * r)
                if ln:
                    sp.wait_ge(x_stored[b], ONE + 16 * r)
                load(r, b)

            def store_rows(r, b):
                if ln:
                    sp.wait_ge(x_ready, ONE + G * (2 * r + b) + G)
                    sp.dma_start(xo_v[2 * r + b], x[:, b, :, :]).then_inc(x_stored[b], 16)

            def store_f1(r, b):
                sp.wait_ge(f1_ready, ONE + 2 * r + b + 1)
                sp.dma_start(f1_v[2 * r + b], f1out[0:H, :].bitcast(F32)).then_inc(f1_stored, 16)

            def store_values(r, b, c):
                g = 2 * r + b
                sp.wait_ge(low_ready[c % 2], ONE + 2 * g + c // 2 + 1)
                sp.dma_start(v_v[G * g + c], vh[c % 2][:, :, :, :, :].rearrange("p h k s d -> p (h k s d)"))\
                    .then_inc(v_stored[c % 2], 16)

            def step(r, b, left):
                if left >= 3:
                    reload(*later(r, b, 3))
                store_values(r, b, 0)
                store_values(r, b, 1)
                if left >= 2:
                    store_rows(*later(r, b, 2))
                if left >= 1:
                    store_f1(*later(r, b, 1))
                store_values(r, b, 2)
                store_values(r, b, 3)

            for kc in range(KC):
                dst = w_sb[:, kc, :]
                sp.dma_start(dst if len(w[kc].shape) == 2 else dst.rearrange("p (h o) -> p h o", h=H), w[kc])\
                    .then_inc(w_loaded, 16)
            for k, a in enumerate((a_src, a_dst)):
                dst = a_bc[:, k, :] if len(a.shape) == 1 else a_bc[:, k, :].rearrange("p (h o) -> p h o", h=H)
                sp.dma_start(dst, a.partition_broadcast(P)).then_inc(a_loaded, 16)
            load(0, 0)
            load(0, 1)
            store_rows(0, 0)
            reload(1, 0)
            store_rows(0, 1)
            store_f1(0, 0)
            with sp.Fori(0, NG // 2 - 2) as r:
                for b in range(2):
                    step(r, b, 3)
            for g in range(NG - 4, NG):
                step(g // 2, g % 2, NG - 1 - g)
            if ln:
                for b in range(2):
                    sp.wait_ge(x_stored[b], ONE + 16 * (NG // 2))
            sp.wait_ge(f1_stored, ONE + 16 * NG)
            for b in range(2):
                sp.wait_ge(v_stored[b], ONE + 16 * (NC // 2))

        @block.vector
        def _(dve):
            nc.vector.memset(lnscale[:, :], math.log(VSCALE)).then_inc(rem_ready, 1)
            dve.wait_ge(w_loaded, ONE + 16 * KC)
            dve.wait_ge(a_loaded, ONE + 32)
            for k in range(2):
                nc.vector.tensor_tensor(wa_tmp[:, :, :], w_sb[:, :, :],
                                        a_bc[:, k:k + 1, :].to_broadcast([P, KC, F]), ALU.mult).then_inc(wa_step, 1)
                dve.wait_ge(wa_step, ONE + 2 * k + 1)
                nc.vector.tensor_reduce(wa[:, :, k * H:(k + 1) * H],
                                        wa_tmp[:, :, :].rearrange("p k (h o) -> p k h o", h=H), AX.X, ALU.add)\
                    .then_inc(wa_step, 1)
                dve.wait_ge(wa_step, ONE + 2 * k + 2)

            def start_norm(r, b):
                if not ln:
                    return
                g = 2 * r + b
                dve.wait_ge(x_loaded[b], ONE + LOADS * r + LOADS)
                xg, og = x[:, b, :, :], o[:, b, :, :]
                if elu:
                    split_elu(nc, dve, g, xg, og, neg, eluw)
                else:
                    nc.vector.tensor_tensor(xg, og, xg, ALU.add).then_inc(eluw["added"], 2)

            def moments(r, b):
                if not ln:
                    return
                g = 2 * r + b
                if elu:
                    join_elu(nc, dve, g, x[:, b, :, :], neg, eluw)
                else:
                    dve.wait_ge(eluw["added"], ONE + 2 * g + 2)
                norm.moments(dve, g, x, b)

            def finish_norm(r, b):
                if ln:
                    norm.finish(dve, 2 * r + b, x, b)

            def f1_rows(r, b):
                g = 2 * r + b
                dve.wait_ge(frows_ready, ONE + g + 1)
                dve.wait_ge(f1_stored, ONE + 16 * g)
                nc.vector.tensor_scalar(f1out[:, :], frows[:, :].bitcast(I32), -2, None, ALU.bitwise_and).then_inc(f1_ready, 1)

            def factors(r, b):
                g = 2 * r + b
                dve.wait_ge(cols_ready, ONE + g + 1)
                f2 = f12[:, bass.ds(G * g, G), H:2 * H]
                k = kexp[:, bass.ds(G * g, G), :, :]
                nc.vector.tensor_scalar(shifted[:, :, 0, :], f2, 1.0 / LN2, ROUNDER, ALU.mult, ALU.add).then_inc(rho_step, 1)
                nc.vector.tensor_scalar(shifted[:, :, 1, :], f2, SLOPE / LN2, ROUNDER, ALU.mult, ALU.add).then_inc(rho_step, 1)
                nc.vector.tensor_scalar(f2low[:, :, :], f2, SLOPE, None, ALU.mult).then_inc(rho_step, 1)
                dve.wait_ge(rho_step, ONE + 4 * g + 3)
                nc.vector.tensor_scalar(k, shifted[:, :, :, :], -ROUNDER, None, ALU.add).then_inc(rho_step, 1)
                dve.wait_ge(rho_step, ONE + 4 * g + 4)
                dve.wait_ge(rho_ready, ONE + g)
                nc.vector.scalar_tensor_tensor(rem[:, :, 0, :], k[:, :, 0, :], -LN2, f2, ALU.mult, ALU.add).then_inc(rem_ready, 1)
                nc.vector.scalar_tensor_tensor(rem[:, :, 1, :], k[:, :, 1, :], -LN2, f2low[:, :, :], ALU.mult, ALU.add)\
                    .then_inc(rem_ready, 1)

            def values(r, b, c):
                g, s = 2 * r + b, c % 2
                dve.wait_ge(high_ready[s], ONE + 2 * g + c // 2)
                dve.wait_ge(low_ready[s], ONE + 2 * g + c // 2)
                nc.vector.tensor_copy(vf[s][:, :, :, D:D + 1],
                                      rho[:, c, :, :].rearrange("p k (h o) -> p h k o", o=1)).then_inc(v_ready[c], 1)
                dve.wait_ge(wx_done, ONE + G * g + c + 1)
                for k in range(2):
                    nc.vector.tensor_tensor(vf[s][:, :, k, 0:D], pW[c][:, :].rearrange("p (h o) -> p h o", h=H),
                                            rho[:, c, k, :].rearrange("p (h o) -> p h o", o=1).to_broadcast([P, H, D]), ALU.mult)\
                        .then_inc(v_ready[c], 1)

            def step(r, b, left):
                if left >= 2:
                    start_norm(*later(r, b, 2))
                factors(r, b)
                if left >= 2:
                    moments(*later(r, b, 2))
                dve.wait_ge(rho_ready, ONE + 2 * r + b + 1)
                values(r, b, 0)
                values(r, b, 1)
                if left >= 2:
                    finish_norm(*later(r, b, 2))
                if left >= 1:
                    f1_rows(*later(r, b, 1))
                values(r, b, 2)
                values(r, b, 3)

            for b in range(2):
                start_norm(0, b)
                moments(0, b)
                finish_norm(0, b)
            f1_rows(0, 0)
            with dve.Fori(0, NG // 2 - 1) as r:
                for b in range(2):
                    step(r, b, 2)
            for b in range(2):
                step(NG // 2 - 1, b, 1 - b)
            for s in range(2):
                dve.wait_ge(high_ready[s], ONE + NC // 2)
                dve.wait_ge(low_ready[s], ONE + NC // 2)
            nc.vector.tensor_reduce(kmax[:, :], kexp[:, :, :, :].rearrange("p c k h -> p (k h) c"), AX.X, ALU.max).then_inc(k_step, 1)
            dve.wait_ge(k_turned, ONE + 1)
            nc.vector.tensor_reduce(khead[:, :], pR[:, 0:P], AX.X, ALU.max).then_inc(k_step, 1)
            dve.wait_ge(k_step, ONE + 2)
            nc.vector.tensor_copy(kspread[:, :], khead[:, :].to_broadcast([2 * H, P])).then_inc(k_step, 1)
            dve.wait_ge(k_spread, ONE + 1)
            nc.vector.tensor_copy(ktop[:, :], pC[:, 0, :]).then_inc(k_step, 1)
            dve.wait_ge(k_step, ONE + 4)
            k = kexp[:, :, :, :].rearrange("p c k h -> p c (k h)")
            nc.vector.tensor_tensor(k, k, ktop[:, :].rearrange("p (o m) -> p o m", o=1).to_broadcast([P, NC, 2 * H]), ALU.subtract)\
                .then_inc(k_step, 1)
            nc.vector.tensor_tensor(dtop[:, :], ktop[:, 0:H], ktop[:, H:2 * H], ALU.subtract).then_inc(rf_step, 1)
            f1 = f12[:, :, 0:H]
            nc.vector.tensor_scalar(fdiff, f1, 1.0 - SLOPE, None, ALU.mult).then_inc(rf_step, 1)
            dve.wait_ge(rf_step, ONE + 2)
            nc.vector.scalar_tensor_tensor(fdiff, dtop[:, :].rearrange("p (o h) -> p o h", o=1).to_broadcast([P, NC, H]), LN2,
                                           fdiff, ALU.mult, ALU.add).then_inc(rf_step, 1)
            dve.wait_ge(rf_step, ONE + 3)
            for k, m in enumerate((1.0, -1.0)):
                nc.vector.tensor_scalar(rfm[:, :, :, k], fdiff, m, 0.0, ALU.mult, ALU.min).then_inc(rf_step, 1)
            f2 = f12[:, :, H:2 * H]
            nc.vector.tensor_scalar(f2, f2, TINY, None, ALU.add).then_inc(rf_step, 1)
            dve.wait_ge(rf_step, ONE + 6)
            nc.vector.tensor_scalar(f2.bitcast(I32), f2.bitcast(I32), 1, None, ALU.bitwise_or).then_inc(rf_step, 1)
            dve.wait_ge(beta_ready, ONE + 1)
            nc.vector.tensor_scalar(ndelta[:, :, 0:H], beta[:, :, 1, 0:H], -1.0, None, ALU.mult).then_inc(rf_step, 1)

        @block.scalar
        def _(act):
            def exps(r, b):
                if ln and elu:
                    act.wait_ge(eluw["neg"], ONE + 2 * r + b + 1)
                    nc.scalar.activation(neg[:, :, :], neg[:, :, :], ACT.Exp).then_inc(eluw["exp"], 1)

            def rsqrt(r, b):
                if ln:
                    norm.rsqrt(act, 2 * r + b)

            def rows_out(r, b):
                for c in range(G):
                    if c == 0 and not (isinstance(r, int) and r == 0):
                        act.wait_ge(wx_done, ONE + G * (2 * r + b) - G)
                    act.wait_ge(turned[b], ONE + G * r + c + 1)
                    nc.scalar.activation(xT[:, b, c, :, :], pT[c % 2][:, :, :], ACT.Copy).then_inc(xT_ready, 1)

            def scores_out(r, b):
                g = 2 * r + b
                act.wait_ge(pR_done, ONE + g + 1)
                act.wait_ge(pC_done, ONE + g)
                act.wait_ge(f1_ready, ONE + g)
                nc.scalar.activation(frows[:, :], pR, ACT.Copy).then_inc(frows_ready, 1)

            def columns_out(r, b):
                g = 2 * r + b
                act.wait_ge(pC_done, ONE + g + 1)
                nc.scalar.activation(f12[:, bass.ds(G * g, G), 0:2 * H], pC, ACT.Copy).then_inc(cols_ready, 1)

            def factors(r, b):
                g = 2 * r + b
                act.wait_ge(rem_ready, ONE + 2 * g + 3)
                act.wait_ge(v_ready[G - 1], ONE + 3 * g)
                nc.scalar.activation(rho[:, :, :, :], rem[:, :, :, :], ACT.Exp, bias=lnscale[:, 0:1]).then_inc(rho_ready, 1)

            def high(r, b, c):
                g, s = 2 * r + b, c % 2
                act.wait_ge(v_stored[s], ONE + 16 * (2 * g + c // 2))
                act.wait_ge(v_ready[c], ONE + 3 * g + 3)
                nc.scalar.activation(vh[s][:, :, :, 0, :], vf[s][:, :, :, :], ACT.Copy).then_inc(high_ready[s], 1)

            def step(r, b, left):
                if left >= 1:
                    rows_out(*later(r, b, 1))
                if left >= 2:
                    exps(*later(r, b, 2))
                factors(r, b)
                if left >= 2:
                    rsqrt(*later(r, b, 2))
                high(r, b, 0)
                high(r, b, 1)
                if left >= 1:
                    scores_out(*later(r, b, 1))
                high(r, b, 2)
                high(r, b, 3)
                if left >= 1:
                    columns_out(*later(r, b, 1))

            exps(0, 0)
            rsqrt(0, 0)
            rows_out(0, 0)
            exps(0, 1)
            rsqrt(0, 1)
            scores_out(0, 0)
            columns_out(0, 0)
            with act.Fori(0, NG // 2 - 1) as r:
                for b in range(2):
                    step(r, b, 2)
            for b in range(2):
                step(NG // 2 - 1, b, 1 - b)
            act.wait_ge(k_step, ONE + 5)
            nc.scalar.activation(beta[:, :, :, 0:H], kexp[:, :, :, :], ACT.Exp, scale=LN2).then_inc(beta_ready, 1)
            act.wait_ge(rf_step, ONE + 7)
            nc.scalar.activation(rowf[:, :, 0:2 * H], rfm.rearrange("p c h k -> p c (h k)"), ACT.Exp).then_inc(rf_ready, 1)

        @block.gpsimd
        def _(pool):
            with pool.Fori(0, NC // 2) as t:
                for s in range(2):
                    pool.wait_ge(high_ready[s], ONE + t + 1)
                    nc.gpsimd.tensor_tensor(vh[s][:, :, :, 1, :], vf[s][:, :, :, :], vh[s][:, :, :, 0, :], ALU.subtract)\
                        .then_inc(low_ready[s], 1)

        @block.tensor
        def _(pe):
            def turn(r, b):
                g = 2 * r + b
                for c in range(G):
                    if ln:
                        pe.wait_ge(x_ready, ONE + G * g + c + 1)
                    elif c == 0:
                        pe.wait_ge(x_loaded[b], ONE + LOADS * r + LOADS)
                    if c < 2:
                        pe.wait_ge(xT_ready, ONE + G * g)
                    else:
                        pe.wait_ge(xT_ready, ONE + G * g + c - 1)
                    for kc in range(KC):
                        last = nc.tensor.transpose(pT[c % 2][:, kc, :], x[:, b, c, kc * P:(kc + 1) * P], ident[:, :])
                    last.then_inc(turned[b], 1)

            def scores(r, b):
                g = 2 * r + b
                pe.wait_ge(xT_ready, ONE + G * g + G)
                pe.wait_ge(frows_ready, ONE + g)
                for kc in range(KC):
                    last = nc.tensor.matmul(pR, wa[:, kc, :], xT[:, b, :, kc, :], start=kc == 0, stop=kc == KC - 1)
                last.then_inc(pR_done, 1)

            def columns(r, b):
                g = 2 * r + b
                pe.wait_ge(frows_ready, ONE + g + 1)
                pe.wait_ge(cols_ready, ONE + g)
                for c in range(G):
                    last = nc.tensor.matmul(pC[:, c, :], frows[:, c * P:(c + 1) * P], ident[0:2 * H, 0:2 * H],
                                            start=True, stop=True)
                last.then_inc(pC_done, 1)

            def products(r, b, c):
                pe.wait_ge(v_ready[c], ONE + 3 * (2 * r + b))
                for kc in range(KC):
                    last = nc.tensor.matmul(pW[c][:, :], xT[:, b, c, kc, :], w_sb[:, kc, :],
                                            start=kc == 0, stop=kc == KC - 1)
                last.then_inc(wx_done, 1)

            def step(r, b, left):
                if left >= 1:
                    turn(*later(r, b, 1))
                products(r, b, 0)
                products(r, b, 1)
                if left >= 1:
                    scores(*later(r, b, 1))
                products(r, b, 2)
                products(r, b, 3)
                if left >= 1:
                    columns(*later(r, b, 1))

            pe.wait_ge(wa_step, ONE + 4)
            turn(0, 0)
            scores(0, 0)
            columns(0, 0)
            with pe.Fori(0, NG // 2 - 1) as r:
                for b in range(2):
                    step(r, b, 1)
            for b in range(2):
                step(NG // 2 - 1, b, 1 - b)
            pe.wait_ge(k_step, ONE + 1)
            nc.tensor.transpose(pR[:, 0:P], kmax[:, :], ident[:, :]).then_inc(k_turned, 1)
            pe.wait_ge(k_step, ONE + 3)
            nc.tensor.matmul(pC[:, 0, :], kspread[:, :], ident[0:2 * H, 0:2 * H], start=True, stop=True).then_inc(k_spread, 1)
    free_semaphores(nc, sems)


def attend(nc, lay, number, mask, mask_dram, v_dram, f1_dram, attn, cols, ident_bf):
    H, D, VW, IB, NIB, CB, CPB = lay.H, lay.D, lay.VW, lay.IB, lay.NIB, lay.CB, lay.CPB
    f12, beta, ndelta, rowf = cols
    D1 = D + 1
    NB = CB // CPB
    BLOCKS = H * NIB
    U = 4
    ROUNDS = NC // U
    ctx = ExitStack()
    with ctx:
        def sb(name, shape, dt):
            return ctx.enter_context(nc.sbuf_tensor(f"{name}_{number}", shape, dt))

        sems = []

        def sem(name):
            sems.append(nc.alloc_semaphore(f"{name}_{number}"))
            return sems[-1]

        val = sb("val", [P, NC, VW], F16)
        f1b = [sb(f"f1b{b}", [P, 1, IB], F32) for b in range(2)]
        odd = [sb(f"odd{k}", [P, IB], BF16) for k in range(U // 2)]
        y = [sb(f"y{u}", [P, IB], BF16) for u in range(U)]
        S = [sb(f"S{b}", [P, IB], BF16) for b in range(2)]
        T = [sb(f"T{b}", [P, IB], BF16) for b in range(2)]
        part = sb("part", [P, 2, NB, CPB, D1], F32)
        res = part[:, 1, :, :, :].rearrange("p n q d -> p (n q d)")[:, 0:CB * D]
        rden = sb("rden", [P, NB, CPB], F32)
        acc = ctx.enter_context(nc.psum_tensor(f"acc_{number}", [P, NB, 512], F32))

        v_loaded, v_last_loaded = sem("val_loaded"), sem("val_last_loaded")
        f1_loaded = [sem(f"f1_loaded{b}") for b in range(2)]
        odd_loaded = [sem(f"odd_loaded{k}") for k in range(U // 2)]
        y_ready = [sem(f"y_ready{u}") for u in range(U)]
        z_ready = [sem(f"z_ready{u}") for u in range(U)]
        s_ready = [sem(f"s_ready{u}") for u in range(U)]
        t_ready = [sem(f"t_ready{u}") for u in range(U)]
        st_used = [sem(f"st_used{u}") for u in range(U)]
        acc_read, sum_ready, rden_ready = sem("acc_read"), sem("sum_ready"), sem("rden_ready")
        res_ready, res_stored = sem("res_ready"), sem("res_stored")
        start_at_one(nc, sems)
        block = ctx.enter_context(nc.Block())

        v_v = v_dram[:, 0:H * VW].rearrange("(q c p) m -> q p c m", c=U, p=P)
        out_v = attn.rearrange("(b c p) f -> b p c f", c=CB, p=P)

        @block.sync
        def _(sp):
            def f1_load(h, ib, b):
                sp.dma_start(f1b[b][:, :, :], f1_dram[bass.ds(h, 1), ib * IB:(ib + 1) * IB].partition_broadcast(P))\
                    .then_inc(f1_loaded[b], 16)

            def v_load(h, q):
                sp.dma_start(val[:, bass.ds(q * U, U), :], v_v[q][:, :, bass.ds(h * VW, VW)])\
                    .then_inc(v_last_loaded if isinstance(q, int) and q == ROUNDS - 1 else v_loaded, 16)

            def odd_loads(m, ib, jq):
                for k in range(U // 2):
                    sp.wait_ge(z_ready[2 * k + 1], ONE + m * ROUNDS + jq)
                    sp.dma_start(odd[k][:, :], mask_dram[2 * jq + k][:, ib * IB:(ib + 1) * IB])\
                        .then_inc(odd_loaded[k], 16)

            def next_values(h, m, q):
                for u in range(U):
                    sp.wait_ge(st_used[u], ONE + m * ROUNDS + q + 1)
                v_load(h + 1, q)

            def store(h, ib, m):
                sp.wait_ge(res_ready, ONE + m + 1)
                sp.dma_start(out_v[ib][:, :, bass.ds(h * D, D)], res.rearrange("p (c d) -> p c d", c=CB)).then_inc(res_stored, 16)

            def head(h, first, last):
                for ib in range(NIB):
                    m = h * NIB + ib
                    odd_loads(m, ib, 1)
                    if not (first and ib == 0):
                        if ib == 0:
                            next_values(h - 1, m - 1, ROUNDS - 1)
                            store(h - 1, NIB - 1, m - 1)
                        else:
                            store(h, ib - 1, m - 1)
                        if not (last and ib == NIB - 1):
                            for u in range(U):
                                sp.wait_ge(y_ready[u], ONE + ROUNDS * m)
                            if ib == NIB - 1:
                                f1_load(h + 1, 0, 0)
                            else:
                                f1_load(h, ib + 1, (ib + 1) % 2)
                    with sp.Fori(2, ROUNDS) as jq:
                        odd_loads(m, ib, jq)
                        if ib == NIB - 1 and not last:
                            next_values(h, m, jq - 2)
                    if not (last and ib == NIB - 1):
                        odd_loads(m + 1, (ib + 1) % NIB, 0)
                        if ib == NIB - 1:
                            next_values(h, m, ROUNDS - 2)

            f1_load(0, 0, 0)
            odd_loads(0, 0, 0)
            for q in range(ROUNDS):
                v_load(0, q)
            f1_load(0, 1, 1)
            head(0, True, False)
            with sp.Fori(1, H - 1) as h:
                head(h, False, False)
            head(H - 1, False, True)
            store(H - 1, NIB - 1, BLOCKS - 1)
            sp.wait_ge(res_stored, ONE + 16 * BLOCKS)

        @block.scalar
        def _(act):
            AHEAD = 2

            def sign(m, s, jq, u):
                h, R = m // NIB, m * ROUNDS + jq
                act.wait_ge(s_ready[u], ONE + R)
                act.wait_ge(t_ready[u], ONE + R)
                nc.scalar.activation(y[u][:, :], f1b[s][:, 0, :], ACT.Sign, bias=f12[:, U * jq + u, bass.ds(H + h, 1)])\
                    .then_inc(y_ready[u], 1)

            def t_part(m, jq):
                h, R, u = m // NIB, m * ROUNDS + jq, U - 1
                act.wait_ge(z_ready[u], ONE + R + 1)
                act.wait_ge(st_used[u - 2], ONE + R + 1)
                nc.scalar.activation(T[u % 2][:, :], y[u][:, :], ACT.Relu, scale=ndelta[:, U * jq + u, bass.ds(h, 1)])\
                    .then_inc(t_ready[u], 1)

            def rounds(m, s, last):
                for u in range(AHEAD, U):
                    sign(m, s, 0, u)
                with act.Fori(1, ROUNDS) as jq:
                    for u in range(AHEAD):
                        sign(m, s, jq, u)
                    t_part(m, jq - 1)
                    for u in range(AHEAD, U):
                        sign(m, s, jq, u)
                if not last:
                    act.wait_ge(f1_loaded[1 - s], ONE + 16 * ((m + 1) // 2) + 16)
                    for u in range(AHEAD):
                        sign(m + 1, 1 - s, 0, u)
                t_part(m, ROUNDS - 1)

            act.wait_ge(f1_loaded[0], ONE + 16)
            for u in range(AHEAD):
                sign(0, 0, 0, u)
            with act.Fori(0, BLOCKS // 2 - 1) as m2:
                for s in range(2):
                    rounds(2 * m2 + s, s, False)
            for s in range(2):
                rounds(BLOCKS - 2 + s, s, s == 1)

        @block.vector
        def _(dve):
            def masked(m, jq, u):
                ib, R = m % NIB, m * ROUNDS + jq
                if u % 2:
                    dve.wait_ge(odd_loaded[u // 2], ONE + 16 * R + 16)
                    chunk = odd[u // 2][:, :]
                else:
                    chunk = mask[:, 2 * jq + u // 2, bass.ds(ib * IB, IB)]
                dve.wait_ge(y_ready[u], ONE + R + 1)
                nc.vector.tensor_tensor(y[u][:, :], y[u][:, :], chunk, ALU.mult).then_inc(z_ready[u], 1)

            def matrices(m, jq, u):
                h, R = m // NIB, m * ROUNDS + jq
                dve.wait_ge(z_ready[u], ONE + R + 1)
                dve.wait_ge(st_used[(u + 2) % U], ONE + R + u // 2)
                nc.vector.tensor_scalar(S[u % 2][:, :], y[u][:, :], 0.0, beta[:, U * jq + u, 0, bass.ds(h, 1)],
                                        ALU.max, ALU.mult).then_inc(s_ready[u], 1)
                if u < U - 1:
                    nc.vector.tensor_scalar(T[u % 2][:, :], y[u][:, :], 0.0, ndelta[:, U * jq + u, bass.ds(h, 1)],
                                            ALU.min, ALU.mult).then_inc(t_ready[u], 1)

            def half(m, jq, k, follows):
                for u in (2 * k, 2 * k + 1):
                    if u < U - 1:
                        masked(m, jq, u + 1)
                    elif follows is not None:
                        masked(*follows, 0)
                    matrices(m, jq, u)

            def read_sums(m):
                h, ib = m // NIB, m % NIB
                for u in range(U):
                    dve.wait_ge(st_used[u], ONE + ROUNDS * m + ROUNDS)
                dve.wait_ge(res_stored, ONE + 16 * m)
                for k in range(2):
                    nc.vector.tensor_tensor(part[:, k, :, :, :],
                                            acc[:, :, 0:CPB * 2 * D1].rearrange("p n (q k d) -> p k n q d", q=CPB, k=2)[:, k],
                                            rowf[:, bass.ds(ib * CB, CB), bass.ds(2 * h + k, 1)]
                                            .rearrange("p (n q) o -> p n q o", q=CPB)
                                            .to_broadcast([P, NB, CPB, D1]), ALU.mult).then_inc(acc_read, 1)

            def invert(m):
                dve.wait_ge(sum_ready, ONE + m + 1)
                nc.vector.reciprocal(rden[:, :, :], part[:, 0, :, :, D]).then_inc(rden_ready, 1)

            def rest_of(m, follows):
                with dve.Fori(1, ROUNDS - 1) as jq:
                    half(m, jq, 0, None)
                    half(m, jq, 1, (m, jq + 1))
                half(m, ROUNDS - 1, 0, None)
                half(m, ROUNDS - 1, 1, follows)

            masked(0, 0, 0)
            half(0, 0, 0, None)
            half(0, 0, 1, (0, 1))
            with dve.Fori(0, BLOCKS - 1) as m:
                rest_of(m, (m + 1, 0))
                masked(m + 1, 0, 1)
                matrices(m + 1, 0, 0)
                read_sums(m)
                masked(m + 1, 0, 2)
                matrices(m + 1, 0, 1)
                half(m + 1, 0, 1, (m + 1, 1))
                invert(m)
            rest_of(BLOCKS - 1, None)
            read_sums(BLOCKS - 1)
            invert(BLOCKS - 1)

        @block.gpsimd
        def _(pool):
            with pool.Fori(0, BLOCKS) as m:
                pool.wait_ge(acc_read, ONE + 2 * m + 2)
                nc.gpsimd.tensor_tensor(part[:, 0, :, :, :], part[:, 0, :, :, :], part[:, 1, :, :, :], ALU.add)\
                    .then_inc(sum_ready, 1)
                pool.wait_ge(rden_ready, ONE + m + 1)
                nc.gpsimd.tensor_tensor(res.rearrange("p (n q d) -> p n q d", n=NB, q=CPB), part[:, 0, :, :, 0:D],
                                        rden[:, :, :].rearrange("p n (q o) -> p n q o", o=1)
                                        .to_broadcast([P, NB, CPB, D]), ALU.mult).then_inc(res_ready, 1)

        @block.tensor
        def _(pe):
            def sums(m, jq):
                R = m * ROUNDS + jq
                for u in range(U):
                    for k, (M, ready) in enumerate(((S, s_ready), (T, t_ready))):
                        pe.wait_ge(ready[u], ONE + R + 1)
                        for c in range(CB):
                            at = (2 * (c % CPB) + k) * D1
                            for part_of in range(2):
                                v0 = (2 * k + part_of) * D1
                                last = nc.tensor.matmul(acc[:, c // CPB, at:at + D1], M[u % 2][:, c * P:(c + 1) * P],
                                                        val[:, U * jq + u, v0:v0 + D1], start=False, stop=False,
                                                        skip_group_check=True)
                    last.then_inc(st_used[u], 1)

            with pe.Fori(0, BLOCKS) as m:
                pe.wait_ge(acc_read, ONE + 2 * m)
                pe.wait_ge(v_loaded, ONE + 16 * (ROUNDS - 1) * (m // NIB + 1))
                for n in range(NB):
                    nc.tensor.matmul(acc[:, n, 510:512], ident_bf[:, :], ident_bf[:, 0:2], start=True, stop=True,
                                     skip_group_check=True)
                with pe.Fori(0, ROUNDS - 1) as jq:
                    sums(m, jq)
                pe.wait_ge(v_last_loaded, ONE + 16 * (m // NIB + 1))
                sums(m, ROUNDS - 1)
    free_semaphores(nc, sems)


def add_self_loops(nc, mask, mask_dram, ident_bf, no_loop):
    EVEN = NC // 2
    ctx = ExitStack()
    with ctx:
        def sb(name, shape, dt):
            return ctx.enter_context(nc.sbuf_tensor(f"{name}_loops", shape, dt))

        sems = []

        def sem(name):
            sems.append(nc.alloc_semaphore(f"{name}_loops"))
            return sems[-1]

        diag = sb("diag", [P, EVEN, P], BF16)
        own = sb("own", [P, 2, EVEN, P], BF16)
        loop = sb("loop", [P, 2, EVEN], F32)
        loaded, own_ready, added, odd_added = sem("loaded"), sem("own_ready"), sem("added"), sem("odd_added")
        counted, stored = sem("counted"), [sem(f"stored{k}") for k in range(2)]
        start_at_one(nc, sems)
        block = ctx.enter_context(nc.Block())

        def move_blocks(queue, first, done):
            for c in range(first, EVEN, 2):
                j = (2 * c + 1) * P
                queue.dma_start(diag[:, c, :], mask_dram[c][:, j:j + P]).then_inc(loaded, 16)
            queue.wait_ge(odd_added, ONE + 1)
            for c in range(first, EVEN, 2):
                j = (2 * c + 1) * P
                queue.dma_start(mask_dram[c][:, j:j + P], diag[:, c, :]).then_inc(done, 16)
            queue.wait_ge(done, ONE + 16 * (EVEN // 2))

        @block.sync
        def _(sp):
            move_blocks(sp, 0, stored[0])

        @block.scalar
        def _(act):
            move_blocks(act, 1, stored[1])

        @block.vector
        def _(dve):
            with dve.Fori(0, EVEN) as c:
                on_diag = mask[:, c, bass.ds(2 * c * P, P)]
                nc.vector.tensor_tensor(own[:, 0, c, :], on_diag, ident_bf[:, :], ALU.mult).then_inc(own_ready, 1)
                dve.wait_ge(own_ready, ONE + c + 1)
                nc.vector.tensor_tensor(on_diag, on_diag, ident_bf[:, :], ALU.max).then_inc(added, 1)
            dve.wait_ge(loaded, ONE + 16 * EVEN)
            ones = ident_bf[:, :].rearrange("p (o j) -> p o j", o=1).to_broadcast([P, EVEN, P])
            nc.vector.tensor_tensor(own[:, 1, :, :], diag[:, :, :], ones, ALU.mult).then_inc(own_ready, 1)
            dve.wait_ge(own_ready, ONE + EVEN + 1)
            nc.vector.tensor_tensor(diag[:, :, :], diag[:, :, :], ones, ALU.max).then_inc(odd_added, 1)
            nc.vector.tensor_reduce(loop[:, :, :], own[:, :, :, :], AX.X, ALU.add).then_inc(counted, 1)
            dve.wait_ge(counted, ONE + 1)
            nc.vector.tensor_scalar(no_loop[:, :].rearrange("p (c k) -> p k c", k=2), loop[:, :, :], -1.0, 1.0,
                                    ALU.mult, ALU.add).then_inc(counted, 1)
    free_semaphores(nc, sems)


def last_layer(nc, x_in, attn, w_self, w_neigh, mask, mask_dram, no_loop, y_dram, x_dram, out, ident, ident_bf):
    number = 3
    G = 4
    NG = NC // G
    ctx = ExitStack()
    with ctx:
        def sb(name, shape, dt):
            return ctx.enter_context(nc.sbuf_tensor(f"{name}_{number}", shape, dt))

        r_bc = sb("r_bc", [P, F], F32)
        x0 = sb("x0", [P, NC], F32)
        s_col = sb("s_col", [P, NC], F32)
        self_product(nc, G, NG, x_in, attn, w_self, w_neigh, y_dram, x_dram, ident, r_bc, x0)
        neighbour_sums(nc, mask, mask_dram, no_loop, ident_bf, x0, s_col)
        combine(nc, G, NG, y_dram, x_dram, r_bc, s_col, out)


def self_product(nc, G, NG, x_in, attn, w_self, w_neigh, y_dram, x_dram, ident, r_bc, x0):
    ctx = ExitStack()
    with ctx:
        def sb(name, shape, dt):
            return ctx.enter_context(nc.sbuf_tensor(f"{name}_3a", shape, dt))

        def ps(name, shape, dt):
            return ctx.enter_context(nc.psum_tensor(f"{name}_3a", shape, dt))

        sems = []

        def sem(name):
            sems.append(nc.alloc_semaphore(f"{name}_3a"))
            return sems[-1]

        w_rows = sb("w_rows", [P, 2, KC, F], F32)
        wT = sb("wT", [P, KC, F], F32)
        rn = sb("rn", [P, KC], F32)
        rn_b = sb("rn_b", [P, KC, P], F32)
        x = sb("x", [P, 2, G, F], F32)
        o = sb("o", [P, 2, G, F], F32)
        xT = w_rows[:, :, :, :].rearrange("p b c (k i) -> p b c k i", i=P)
        neg = sb("neg", [P, G, F], F32)
        ys = sb("ys", [P, G, F], F32)
        norm = Norm(nc, sb, sem, G)
        eluw = {k: sem(f"elu_{k}") for k in ("neg", "exp", "added")}
        pT = [ps(f"pT{b}", [P, KC, P], F32) for b in range(2)]
        pW = [ps(f"pW{c}", [P, F], F32) for c in range(G)]
        w_loaded, rn_ready, rnb_ready, r_done, r_copied = (sem(n) for n in ("w_loaded", "rn_ready", "rnb_ready", "r_done", "r_copied"))
        w_turned, wT_ready = sem("w_turned"), sem("wT_ready")
        x_loaded = [sem(f"x_loaded{b}") for b in range(2)]
        x_stored = [sem(f"x_stored{b}") for b in range(2)]
        x0_ready = sem("x0_ready")
        turned = [sem(f"turned{b}") for b in range(2)]
        xT_ready, y_done = sem("xT_ready"), sem("y_done")
        y_copied = [sem(f"y_copied{c}") for c in range(G)]
        y_stored = [sem(f"y_stored{c}") for c in range(G)]
        start_at_one(nc, sems)
        block = ctx.enter_context(nc.Block())
        x_v = x_in.rearrange("(g c p) f -> g p c f", c=G, p=P)
        o_v = attn.rearrange("(g c p) f -> g p c f", c=G, p=P)
        xo_v = x_dram.rearrange("(g c p) f -> g p c f", c=G, p=P)
        y_v = y_dram.rearrange("(c p) f -> c p f", p=P)

        def later(r, b, k):
            return r + (b + k) // 2, (b + k) % 2

        @block.sync
        def _(sp):
            def load(r, b):
                sp.dma_start(x[:, b, :, :], x_v[2 * r + b]).then_inc(x_loaded[b], 16)
                sp.dma_start(o[:, b, :, :], o_v[2 * r + b]).then_inc(x_loaded[b], 16)

            def reload(r, b):
                sp.wait_ge(turned[b], ONE + G * r)
                sp.wait_ge(x_stored[b], ONE + 16 * r)
                load(r, b)

            def store_rows(r, b):
                sp.wait_ge(x0_ready, ONE + 2 * r + b + 1)
                sp.dma_start(xo_v[2 * r + b], x[:, b, :, :]).then_inc(x_stored[b], 16)

            def step(r, b, left):
                if left >= 3:
                    reload(*later(r, b, 3))
                for c in range(G):
                    if c == 2 and left >= 2:
                        store_rows(*later(r, b, 2))
                    sp.wait_ge(y_copied[c], ONE + 2 * r + b + 1)
                    sp.dma_start(y_v[G * (2 * r + b) + c], ys[:, c, :]).then_inc(y_stored[c], 16)

            for k, w in enumerate((w_self, w_neigh)):
                sp.dma_start(w_rows[:, k, :, :], w.rearrange("(c p) f -> p c f", p=P)).then_inc(w_loaded, 16)
            load(0, 0)
            load(0, 1)
            store_rows(0, 0)
            reload(1, 0)
            store_rows(0, 1)
            with sp.Fori(0, NG // 2 - 2) as r:
                for b in range(2):
                    step(r, b, 3)
            for g in range(NG - 4, NG):
                step(g // 2, g % 2, NG - 1 - g)
            for c in range(G):
                sp.wait_ge(y_stored[c], ONE + 16 * NG)
            for b in range(2):
                sp.wait_ge(x_stored[b], ONE + 16 * (NG // 2))

        @block.vector
        def _(dve):
            dve.wait_ge(w_loaded, ONE + 32)
            nc.vector.tensor_reduce(rn[:, :], w_rows[:, 1, :, :], AX.X, ALU.add).then_inc(rn_ready, 1)
            dve.wait_ge(rn_ready, ONE + 1)
            nc.vector.tensor_copy(rn_b[:, :, :], rn[:, :].rearrange("p (c o) -> p c o", o=1).to_broadcast([P, KC, P]))\
                .then_inc(rnb_ready, 1)

            def layernorm(r, b):
                g = 2 * r + b
                dve.wait_ge(x_loaded[b], ONE + 32 * r + 32)
                split_elu(nc, dve, g, x[:, b, :, :], o[:, b, :, :], neg, eluw)
                join_elu(nc, dve, g, x[:, b, :, :], neg, eluw)
                norm.rows(dve, g, x, b)
                dve.wait_ge(norm.ready, ONE + G * g + G)
                nc.vector.tensor_copy(x0[:, bass.ds(G * g, G)], x[:, b, :, 0]).then_inc(x0_ready, 1)

            with dve.Fori(0, NG // 2) as r:
                for b in range(2):
                    layernorm(r, b)

        @block.scalar
        def _(act):
            def rsqrt(r, b):
                act.wait_ge(eluw["neg"], ONE + 2 * r + b + 1)
                nc.scalar.activation(neg[:, :, :], neg[:, :, :], ACT.Exp).then_inc(eluw["exp"], 1)
                norm.rsqrt(act, 2 * r + b)

            def rows_out(r, b):
                for c in range(G):
                    if c == 0 and not (isinstance(r, int) and r == 0):
                        act.wait_ge(y_done, ONE + G * (2 * r + b) - G)
                    act.wait_ge(turned[b], ONE + G * r + c + 1)
                    nc.scalar.activation(xT[:, b, c, :, :], pT[c % 2][:, :, :], ACT.Copy).then_inc(xT_ready, 1)

            def step(r, b, left):
                g = 2 * r + b
                if left >= 1:
                    rows_out(*later(r, b, 1))
                if left >= 2:
                    rsqrt(*later(r, b, 2))
                for c in range(G):
                    act.wait_ge(y_done, ONE + G * g + c + 1)
                    act.wait_ge(y_stored[c], ONE + 16 * g)
                    nc.scalar.activation(ys[:, c, :], pW[c][:, :], ACT.Copy).then_inc(y_copied[c], 1)

            for c in range(KC):
                act.wait_ge(w_turned, ONE + c + 1)
                nc.scalar.activation(wT[:, c, :], pT[c % 2][:, :, :].rearrange("p c f -> p (c f)"), ACT.Copy).then_inc(wT_ready, 1)
            act.wait_ge(r_done, ONE + 1)
            nc.scalar.activation(r_bc[:, :], pW[0][:, :], ACT.Copy).then_inc(r_copied, 1)
            rsqrt(0, 0)
            rows_out(0, 0)
            rsqrt(0, 1)
            with act.Fori(0, NG // 2 - 1) as r:
                for b in range(2):
                    step(r, b, 2)
            for b in range(2):
                step(NG // 2 - 1, b, 1 - b)

        @block.tensor
        def _(pe):
            def turn(r, b):
                g = 2 * r + b
                for c in range(G):
                    pe.wait_ge(norm.ready, ONE + G * g + c + 1)
                    if c < 2:
                        pe.wait_ge(xT_ready, ONE + G * g)
                    else:
                        pe.wait_ge(xT_ready, ONE + G * g + c - 1)
                    for kc in range(KC):
                        last = nc.tensor.transpose(pT[c % 2][:, kc, :], x[:, b, c, kc * P:(kc + 1) * P], ident[:, :])
                    last.then_inc(turned[b], 1)

            def step(r, b, left):
                g = 2 * r + b
                if left >= 1:
                    turn(*later(r, b, 1))
                for c in range(G):
                    if c == 0:
                        pe.wait_ge(xT_ready, ONE + G * g + G)
                    pe.wait_ge(y_copied[c], ONE + g)
                    for kc in range(KC):
                        last = nc.tensor.matmul(pW[c][:, :], xT[:, b, c, kc, :], wT[:, kc, :],
                                                start=kc == 0, stop=kc == KC - 1)
                    last.then_inc(y_done, 1)

            pe.wait_ge(w_loaded, ONE + 32)
            for c in range(KC):
                if c >= 2:
                    pe.wait_ge(wT_ready, ONE + c - 1)
                for k in range(KC):
                    last = nc.tensor.transpose(pT[c % 2][:, k, :], w_rows[:, 0, k, c * P:(c + 1) * P], ident[:, :])
                last.then_inc(w_turned, 1)
            pe.wait_ge(rnb_ready, ONE + 1)
            for c in range(KC):
                last = nc.tensor.matmul(pW[0][:, c * P:(c + 1) * P], rn_b[:, c, :], ident[:, :], start=True, stop=True)
            last.then_inc(r_done, 1)
            pe.wait_ge(r_copied, ONE + 1)
            pe.wait_ge(wT_ready, ONE + KC)
            turn(0, 0)
            with pe.Fori(0, NG // 2 - 1) as r:
                for b in range(2):
                    step(r, b, 1)
            for b in range(2):
                step(NG // 2 - 1, b, 1 - b)
    free_semaphores(nc, sems)


def neighbour_sums(nc, mask, mask_dram, no_loop, ident_bf, x0, s_col):
    ctx = ExitStack()
    with ctx:
        def sb(name, shape, dt):
            return ctx.enter_context(nc.sbuf_tensor(f"{name}_3b", shape, dt))

        sems = []

        def sem(name):
            sems.append(nc.alloc_semaphore(f"{name}_3b"))
            return sems[-1]

        parts = sb("parts", [P, NC, 3], BF16)
        rest = sb("rest", [P, 2, NC], F32)
        odd = [sb(f"odd{b}", [P, N], BF16) for b in range(4)]
        acc = ctx.enter_context(nc.psum_tensor("acc_3b", [P, NC, 16], F32))
        split, summed = sem("split"), sem("summed")
        odd_loaded = [sem(f"odd_loaded{b}") for b in range(4)]
        used = [sem(f"used{b}") for b in range(4)]
        start_at_one(nc, sems)
        block = ctx.enter_context(nc.Block())

        @block.sync
        def _(sp):
            with sp.Fori(0, NC // 8) as t:
                for b in range(4):
                    sp.wait_ge(used[b], ONE + t)
                    sp.dma_start(odd[b][:, :], mask_dram[4 * t + b]).then_inc(odd_loaded[b], 16)

        @block.vector
        def _(dve):
            nc.vector.tensor_copy(parts[:, :, 0], x0[:, :]).then_inc(split, 1)
            dve.wait_ge(split, ONE + 1)
            nc.vector.tensor_tensor(rest[:, 0, :], x0[:, :], parts[:, :, 0], ALU.subtract).then_inc(split, 1)
            dve.wait_ge(split, ONE + 2)
            nc.vector.tensor_copy(parts[:, :, 1], rest[:, 0, :]).then_inc(split, 1)
            dve.wait_ge(split, ONE + 3)
            nc.vector.tensor_tensor(rest[:, 1, :], rest[:, 0, :], parts[:, :, 1], ALU.subtract).then_inc(split, 1)
            dve.wait_ge(split, ONE + 4)
            nc.vector.tensor_copy(parts[:, :, 2], rest[:, 1, :]).then_inc(split, 1)
            for b in range(4):
                dve.wait_ge(used[b], ONE + NC // 8)
            nc.vector.tensor_reduce(s_col[:, :], acc[:, :, 0:3], AX.X, ALU.add).then_inc(summed, 1)
            nc.vector.tensor_tensor(rest[:, 0, :], no_loop[:, :], x0[:, :], ALU.mult).then_inc(summed, 1)
            dve.wait_ge(summed, ONE + 2)
            nc.vector.tensor_tensor(s_col[:, :], s_col[:, :], rest[:, 0, :], ALU.subtract).then_inc(summed, 1)

        @block.tensor
        def _(pe):
            def chunk(stationary, j):
                for c in range(NC):
                    last = nc.tensor.matmul(acc[:, c, 0:3], stationary[:, c * P:(c + 1) * P], parts[:, j, :],
                                            start=False, stop=False, skip_group_check=True)
                return last

            nc.tensor.matmul(acc[:, NC - 1, 14:16], ident_bf[:, :], ident_bf[:, 0:2], start=True, stop=True, skip_group_check=True)
            pe.wait_ge(split, ONE + 5)
            with pe.Fori(0, NC // 8) as t:
                for b in range(4):
                    chunk(mask[:, 4 * t + b, :], 8 * t + 2 * b)
                    pe.wait_ge(odd_loaded[b], ONE + 16 * t + 16)
                    chunk(odd[b], 8 * t + 2 * b + 1).then_inc(used[b], 1)
    free_semaphores(nc, sems)


def combine(nc, G, NG, y_dram, x_dram, r_bc, s_col, out):
    ctx = ExitStack()
    with ctx:
        def sb(name, shape, dt):
            return ctx.enter_context(nc.sbuf_tensor(f"{name}_3c", shape, dt))

        sems = []

        def sem(name):
            sems.append(nc.alloc_semaphore(f"{name}_3c"))
            return sems[-1]

        x = sb("x", [P, 2, G, F], F32)
        y = sb("y", [P, 2, G, F], F32)
        norm = Norm(nc, sb, sem, G)
        loaded = [sem(f"loaded{b}") for b in range(2)]
        stored = [sem(f"stored{b}") for b in range(2)]
        y_step, added = sem("y_step"), sem("added")
        start_at_one(nc, sems)
        block = ctx.enter_context(nc.Block())
        x_v = x_dram.rearrange("(g c p) f -> g p c f", c=G, p=P)
        y_v = y_dram.rearrange("(g c p) f -> g p c f", c=G, p=P)
        out_v = out.rearrange("(g c p) f -> g p c f", c=G, p=P)

        @block.sync
        def _(sp):
            with sp.Fori(0, NG // 2) as r:
                for b in range(2):
                    sp.wait_ge(stored[b], ONE + 16 * r)
                    sp.dma_start(x[:, b, :, :], x_v[2 * r + b]).then_inc(loaded[b], 16)
                    sp.dma_start(y[:, b, :, :], y_v[2 * r + b]).then_inc(loaded[b], 16)

        @block.scalar
        def _(act):
            with act.Fori(0, NG // 2) as r:
                for b in range(2):
                    g = 2 * r + b
                    norm.rsqrt(act, g)
                    act.wait_ge(norm.ready, ONE + G * g + G)
                    act.dma_start(out_v[g], x[:, b, :, :]).then_inc(stored[b], 16)
            for b in range(2):
                act.wait_ge(stored[b], ONE + 16 * (NG // 2))

        @block.vector
        def _(dve):
            with dve.Fori(0, NG // 2) as r:
                for b in range(2):
                    g = 2 * r + b
                    dve.wait_ge(loaded[b], ONE + 32 * r + 32)
                    for c in range(G):
                        nc.vector.scalar_tensor_tensor(y[:, b, c, :], r_bc[:, :], s_col[:, bass.ds(G * g + c, 1)],
                                                       y[:, b, c, :], ALU.mult, ALU.add).then_inc(y_step, 1)
                    dve.wait_ge(y_step, ONE + G * g + G)
                    nc.vector.scalar_tensor_tensor(x[:, b, :, :], y[:, b, :, :], 0.0, x[:, b, :, :], ALU.max, ALU.add)\
                        .then_inc(added, 1)
                    dve.wait_ge(added, ONE + g + 1)
                    norm.rows(dve, g, x, b)
    free_semaphores(nc, sems)


def gat_kernel(nc, x, adj, W0, a1, a2, W1, a, W2, a_l, a_r, w_self, w_neigh, out):
    def dram(name, shape, dt):
        return nc.dram_tensor(name, shape, dt, kind="Internal").ap()

    f1_dram = dram("f1_rows", (8, N), F32)
    v_dram = dram("values", (N, 8 * 4 * 65), F16)
    attn = dram("attended", (N, F), F32)
    mask_dram = dram("mask_odd", (NC // 2, P, N), BF16)
    y_dram = dram("self_products", (N, F), F32)
    rows = [dram(f"rows{k}", (N, F), F32) for k in range(2)]

    ctx = ExitStack()
    with ctx:
        def sb(name, shape, dt):
            return ctx.enter_context(nc.sbuf_tensor(name, shape, dt))

        mask = sb("mask", [P, NC // 2, N], BF16)
        f12 = sb("f12", [P, NC, 16], F32)
        beta = sb("beta", [P, NC, 2, 8], BF16)
        rowf = sb("rowf", [P, NC, 16], F32)
        ndelta = sb("ndelta", [P, NC, 8], F32)
        no_loop = sb("no_loop", [P, NC], F32)
        ident = sb("ident", [P, P], F32)
        ident_bf = sb("ident_bf", [P, P], BF16)
        cols = (f12, beta, ndelta, rowf)
        made = ctx.enter_context(nc.semaphore("ident_made"))
        with nc.Block() as block:
            @block.gpsimd
            def _(pool):
                nc.gpsimd.memset(ident[:, :], 0.0).then_inc(made, 1)
                nc.gpsimd.memset(ident_bf[:, :], 0.0).then_inc(made, 1)
                pool.wait_ge(made, 2)
                for m in (ident, ident_bf):
                    nc.gpsimd.affine_select(out=m[:, :], in_=m[:, :], compare_op=ALU.not_equal, fill=1.0, base=0,
                                            pattern=[[-1, P]], channel_multiplier=1).then_inc(made, 1)
                pool.wait_ge(made, 4)

        eight, four = Layer(8), Layer(4)
        load_adjacency(nc, adj, mask, mask_dram, ident_bf)
        w0 = [W0[:, k * P:(k + 1) * P, :].rearrange("h k o -> k h o") for k in range(KC)]
        w1 = [W1[k * P:(k + 1) * P, :] for k in range(KC)]
        w2 = [W2[k * P:(k + 1) * P, :] for k in range(KC)]
        flat = [a1.rearrange("h o -> (h o)"), a2.rearrange("h o -> (h o)")]
        prepare(nc, eight, 0, x, None, False, w0, *flat, None, v_dram, f1_dram, cols, ident)
        attend(nc, eight, 0, mask, mask_dram, v_dram, f1_dram, attn, cols, ident_bf)
        flat = [a[0, :, k * 64:(k + 1) * 64] for k in range(2)]
        prepare(nc, eight, 1, x, attn, False, w1, *flat, rows[0], v_dram, f1_dram, cols, ident)
        attend(nc, eight, 1, mask, mask_dram, v_dram, f1_dram, attn, cols, ident_bf)
        flat = [m.rearrange("h o -> (h o)") for m in (a_l, a_r)]
        prepare(nc, four, 2, rows[0], attn, True, w2, *flat, rows[1], v_dram, f1_dram, cols, ident)
        add_self_loops(nc, mask, mask_dram, ident_bf, no_loop)
        attend(nc, four, 2, mask, mask_dram, v_dram, f1_dram, attn, cols, ident_bf)
        last_layer(nc, rows[1], attn, w_self, w_neigh, mask, mask_dram, no_loop, y_dram, rows[0], out, ident, ident_bf)


_INS = ['x', 'adj', 'L0_gnn_W', 'L0_gnn_a1', 'L0_gnn_a2', 'L1_gnn_W', 'L1_gnn_a', 'L2_gnn_W', 'L2_gnn_a_l', 'L2_gnn_a_r',
        'L3_gnn_w_self', 'L3_gnn_w_neigh']


def kernel(**inputs):
    import numpy as np
    import concourse.bacc as bacc
    from concourse.bass_utils import run_bass_kernel_spmd

    nc = bacc.Bacc("TRN2", target_bir_lowering=False, num_devices=1,
                   dynamic_dma_scratch_size=64)
    arrays, args = {}, []
    for name in _INS:
        a = np.ascontiguousarray(inputs[name])
        arrays[f"in_{name}"] = a
        args.append(nc.dram_tensor(f"in_{name}", a.shape, mybir.dt.from_np(a.dtype), kind="ExternalInput").ap())
    args.append(nc.dram_tensor("out_0", (N, F), F32, kind="ExternalOutput").ap())
    gat_kernel(nc, *args)
    r = run_bass_kernel_spmd(nc, [arrays], core_ids=[0])
    return r.results[0]["out_0"]
```
